# Optimizing a Trainium2 kernel written in Bass

```python
import numpy as np
import jax
import jax.numpy as jnp

def _softmax(x, axis=-1):
    return jax.nn.softmax(x, axis=axis)

def _gelu(x):
    return jax.nn.gelu(x, approximate=True)

def _silu(x):
    return jax.nn.silu(x)

def _sigmoid(x):
    return jax.nn.sigmoid(x)

def _layernorm(x, axis=-1, eps=1e-05):
    m = jnp.mean(x, axis=axis, keepdims=True)
    v = jnp.var(x, axis=axis, keepdims=True)
    return (x - m) / jnp.sqrt(v + eps)

def _scatter_add(tgt, idx, src, axis=0):
    return tgt.at[idx].add(src)

def _segment_sum(src, seg, n):
    return jax.ops.segment_sum(src, seg, n)
kernel_name = 'mk_gnn_resnorm_d2_gnn_r8_33efad'

def setup_inputs(seed: int=0):
    np.random.seed(seed)
    _w = jnp.asarray

    def _rec_inputs():
        import jax
        import jax.numpy as jnp
        _gk = jax.random.key(seed)
        x = -0.000202 + 1 * jax.random.normal(jax.random.fold_in(_gk, 1), (6250, 128), jnp.float32)
        _s = jax.random.randint(jax.random.fold_in(_gk, 2), (100000,), 0, 6250, jnp.int32)
        _d = jax.random.randint(jax.random.fold_in(_gk, 3), (100000,), 0, 6250, jnp.int32)
        _loop = jnp.arange(6250, dtype=jnp.int32)
        src = jnp.concatenate([_s, _d, _loop])
        dst = jnp.concatenate([_d, _s, _loop])
        _o = jnp.argsort(dst, stable=True)
        src = src[_o]
        dst = dst[_o]
        edge_weight = jax.random.uniform(jax.random.fold_in(_gk, 12), (206250,), jnp.float32, 0.0, 0.999998)
        return (x, src, dst, edge_weight)
    x, src, dst, edge_weight = _rec_inputs()

    def _L0_gnn_setup():
        import jax, jax.numpy as jnp
        import numpy as np
        N_NODES = 6250
        N_EDGES = 200000
        D_IN, D_HID, D_OUT = (128, 128, 128)

        def _gcn_conv(x, src, dst, W, b):
            n = x.shape[0]
            h = x @ W.T
            loop = jnp.arange(n)
            src_a = jnp.concatenate([src, loop])
            dst_a = jnp.concatenate([dst, loop])
            deg = jax.ops.segment_sum(jnp.ones_like(dst_a, dtype=h.dtype), dst_a, num_segments=n)
            dinv = jnp.where(deg > 0, jax.lax.rsqrt(deg), 0.0)
            norm = dinv[src_a] * dinv[dst_a]
            msg = h[src_a] * norm[:, None]
            out = jax.ops.segment_sum(msg, dst_a, num_segments=n)
            return out + b
        key = jax.random.key(seed)
        k1, k2, k3, k4, k5, k6, k7 = jax.random.split(key, 7)
        x = jax.random.normal(k1, (N_NODES, D_IN), dtype=jnp.float32)
        src = jax.random.randint(k2, (N_EDGES,), 0, N_NODES)
        dst = jax.random.randint(k3, (N_EDGES,), 0, N_NODES)
        edge_index = jnp.stack([src, dst]).astype(jnp.int64)
        W1 = jax.random.normal(k4, (D_HID, D_IN), dtype=jnp.float32) / np.sqrt(D_IN)
        b1 = jnp.zeros((D_HID,), dtype=jnp.float32)
        W2 = jax.random.normal(k5, (D_OUT, D_HID), dtype=jnp.float32) / np.sqrt(D_HID)
        b2 = jnp.zeros((D_OUT,), dtype=jnp.float32)
        return {'x': x, 'edge_index': edge_index, 'W1': W1, 'b1': b1, 'W2': W2, 'b2': b2}
    _L0_gnn_all = _L0_gnn_setup()
    _L0_gnn_in = {k: v for k, v in _L0_gnn_all.items() if k in ('W1', 'b1', 'W2', 'b2')}
    del _L0_gnn_all

    def _L1_gnn_setup():
        import jax, jax.numpy as jnp
        import numpy as np
        N_NODES = 12500
        N_EDGES = 75000
        C_IN = 128
        C_OUT = 128
        key = jax.random.key(seed)
        k_x, k_ei, k_ew, k_pw, k_pb, k_fw, k_fb = jax.random.split(key, 7)
        x = jax.random.normal(k_x, (N_NODES, C_IN), dtype=jnp.float32)
        edge_index = jax.random.randint(k_ei, (2, N_EDGES), 0, N_NODES, dtype=jnp.int64)
        edge_weight = jax.random.uniform(k_ew, (N_EDGES,), dtype=jnp.float32)
        s1 = 1.0 / np.sqrt(C_IN)
        s2 = 1.0 / np.sqrt(2 * C_IN)
        pool_w = jax.random.uniform(k_pw, (C_IN, C_IN), jnp.float32, -s1, s1)
        pool_b = jax.random.uniform(k_pb, (C_IN,), jnp.float32, -s1, s1)
        final_w = jax.random.uniform(k_fw, (C_OUT, 2 * C_IN), jnp.float32, -s2, s2)
        final_b = jax.random.uniform(k_fb, (C_OUT,), jnp.float32, -s2, s2)
        return {'x': x, 'edge_index': edge_index, 'edge_weight': edge_weight, 'pool_w': pool_w, 'pool_b': pool_b, 'final_w': final_w, 'final_b': final_b}
    _L1_gnn_all = _L1_gnn_setup()
    _L1_gnn_in = {k: v for k, v in _L1_gnn_all.items() if k in ('pool_w', 'pool_b', 'final_w', 'final_b')}
    del _L1_gnn_all
    return {'x': x, 'src': src, 'dst': dst, 'edge_weight': edge_weight, 'L0_gnn_W1': _L0_gnn_in['W1'], 'L0_gnn_b1': _L0_gnn_in['b1'], 'L0_gnn_W2': _L0_gnn_in['W2'], 'L0_gnn_b2': _L0_gnn_in['b2'], 'L1_gnn_pool_w': _L1_gnn_in['pool_w'], 'L1_gnn_pool_b': _L1_gnn_in['pool_b'], 'L1_gnn_final_w': _L1_gnn_in['final_w'], 'L1_gnn_final_b': _L1_gnn_in['final_b']}

def reference(x, src, dst, edge_weight, L0_gnn_W1, L0_gnn_b1, L0_gnn_W2, L0_gnn_b2, L1_gnn_pool_w, L1_gnn_pool_b, L1_gnn_final_w, L1_gnn_final_b):
    import jax
    import jax.numpy as jnp

    def _L0_gnn_ref(x, edge_index, W1, b1, W2, b2):
        import jax, jax.numpy as jnp
        import numpy as np
        N_NODES = 6250
        N_EDGES = 200000
        D_IN, D_HID, D_OUT = (128, 128, 128)

        def _gcn_conv(x, src, dst, W, b):
            n = x.shape[0]
            h = x @ W.T
            loop = jnp.arange(n)
            src_a = jnp.concatenate([src, loop])
            dst_a = jnp.concatenate([dst, loop])
            deg = jax.ops.segment_sum(jnp.ones_like(dst_a, dtype=h.dtype), dst_a, num_segments=n)
            dinv = jnp.where(deg > 0, jax.lax.rsqrt(deg), 0.0)
            norm = dinv[src_a] * dinv[dst_a]
            msg = h[src_a] * norm[:, None]
            out = jax.ops.segment_sum(msg, dst_a, num_segments=n)
            return out + b
        src, dst = (edge_index[0], edge_index[1])
        h = _gcn_conv(x, src, dst, W1, b1)
        h = jax.nn.relu(h)
        out = _gcn_conv(h, src, dst, W2, b2)
        return out

    def _L1_gnn_ref(x, edge_index, edge_weight, pool_w, pool_b, final_w, final_b):
        import jax, jax.numpy as jnp
        import numpy as np
        N_NODES = 12500
        N_EDGES = 75000
        C_IN = 128
        C_OUT = 128
        src, dst = (edge_index[0], edge_index[1])
        msg = x[src] * edge_weight[:, None]
        pooled = jax.nn.relu(msg @ pool_w.T + pool_b)
        aggregate = jax.ops.segment_max(pooled, dst, num_segments=x.shape[0])
        aggregate = jnp.maximum(aggregate, 0.0)
        h = jnp.concatenate([x, aggregate], axis=-1)
        out = jax.nn.relu(h @ final_w.T + final_b)
        return out
    edge_index = jnp.stack([src, dst])
    x = _layernorm(x + _L0_gnn_ref(x, edge_index, L0_gnn_W1, L0_gnn_b1, L0_gnn_W2, L0_gnn_b2), axis=-1)
    x = _layernorm(x + _L1_gnn_ref(x, edge_index, edge_weight, L1_gnn_pool_w, L1_gnn_pool_b, L1_gnn_final_w, L1_gnn_final_b), axis=-1)
    return x

_drawn_inputs = setup_inputs


def setup_inputs(seed=0):
    import zlib

    import numpy as np

    out = dict(_drawn_inputs(seed))
    spreads = {'L0_gnn_b1': (0.0, 0.1), 'L0_gnn_b2': (0.0, 0.1)}
    factors = {'L1_gnn_pool_b': 4.143}
    for name, (base, spread) in spreads.items():
        noise = np.random.default_rng([zlib.crc32(name.encode()), seed]).standard_normal(out[name].shape)
        drawn = base * np.exp(spread * noise) if base else spread * noise
        out[name] = jnp.asarray(drawn.astype(out[name].dtype))
    for name, factor in factors.items():
        out[name] = (out[name] * factor).astype(out[name].dtype)
    return out
```

```python
from contextlib import ExitStack

import concourse.bass as bass
from concourse import mybir

P = 128
F = 128
NODES = 6250
EDGES = 206250
TILES = -(-NODES // P)
NPAD = TILES * P
TAIL = NODES - (TILES - 1) * P
GC = 4
GE = GC * P
SLOTS = 4
ROUNDS = -(-EDGES // (GE * SLOTS))
GROUPS = ROUNDS * SLOTS
CHUNKS = GROUPS * GC
EPAD = GROUPS * GE
BLOCKS = -(-CHUNKS // P)
LASTP = CHUNKS - (BLOCKS - 1) * P
FULL = (BLOCKS - 1) * P * P
ROWS_LEFT = (EDGES - FULL) // P
EDGES_LEFT = EDGES - FULL - ROWS_LEFT * P
HEADS = -(-EDGES // GE)
TG = 7
TURNS = TILES // TG
RESET = -3.3e38
NOWHERE = 1.0e6
EPS = 1e-5

ALU = mybir.AluOpType
ACT = mybir.ActivationFunctionType
AX = mybir.AxisListType
F32 = mybir.dt.float32
BF16 = mybir.dt.bfloat16
I32 = mybir.dt.int32
U32 = mybir.dt.uint32


def program(nc, x, src, dst, edge_weight, w1, b1, w2, b2, pool_w, pool_b, final_w, final_b, out):
    with ExitStack() as ctx:
        def sb(name, shape, dt=F32):
            return ctx.enter_context(nc.sbuf_tensor(name, shape, dt))

        def ps(name, shape, dt=F32):
            return ctx.enter_context(nc.psum_tensor(name, shape, dt))

        def sem(name):
            return ctx.enter_context(nc.semaphore(name))

        table = [nc.dram_tensor(f"table{k}", [NPAD, F], F32, kind="Internal").ap() for k in range(3)]
        scan_rows = [nc.dram_tensor(f"scan_rows{k}", [EPAD, F], F32, kind="Internal").ap() for k in range(3)]
        dst_rows = nc.dram_tensor("dst_rows", [GROUPS, GE], F32, kind="Internal").ap()
        sum_mask = nc.dram_tensor("sum_mask", [CHUNKS, P], BF16, kind="Internal").ap()
        max_mask = nc.dram_tensor("max_mask", [CHUNKS, P], BF16, kind="Internal").ap()

        src_i = sb("src_i", [P, BLOCKS, P], I32)
        dst_i = sb("dst_i", [P, BLOCKS, P], I32)
        prev_i = sb("prev_i", [P, BLOCKS, P], I32)
        src_f = sb("src_f", [P, BLOCKS, P])
        wgt_f = sb("wgt_f", [P, BLOCKS, P])
        dst_f = sb("dst_f", [P, BLOCKS, P])
        smask = sb("smask", [P, BLOCKS, P], BF16)
        mmask = sb("mmask", [P, BLOCKS, P], BF16)
        src_t = sb("src_t", [P, BLOCKS * P + SLOTS * GC], U32)
        wgt_t = sb("wgt_t", [P, BLOCKS * P])

        xin = sb("xin", [P, TILES, F])
        self1 = sb("self1", [P, TILES, F])
        self2 = sb("self2", [P, TILES, F])
        ids_i = sb("ids_i", [P, TILES], I32)
        ids = sb("ids", [P, TILES])
        idh = sb("idh", [P, TILES])
        signs = sb("signs", [P, TILES])
        head_row = sb("head_row", [P, TILES])
        head_idx = sb("head_idx", [P, TILES], U32)
        inner = sb("inner", [P, TILES])
        count = sb("count", [P, TILES + 1])
        indeg = sb("indeg", [P, TILES])
        indeg_i = sb("indeg_i", [P, TILES], I32)
        indeg_r = sb("indeg_r", [P, TILES])
        deg = sb("deg", [P, TILES])
        sdeg = sb("sdeg", [P, TILES])
        dinv = sb("dinv", [P, TILES])
        has = sb("has", [P, TILES])
        dinv_has = sb("dinv_has", [P, TILES])
        last_f = sb("last_f", [P, TILES])
        last_idx = sb("last_idx", [P, TILES + TG], U32)
        heads_i = sb("heads_i", [1, HEADS], I32)
        heads_f = sb("heads_f", [1, HEADS])
        sign_junk = sb("sign_junk", [P, 2, HEADS])
        level = sb("level", [P, 4, GE])
        level_junk = sb("level_junk", [P, GE])

        ident = sb("ident", [P, P])
        shift = sb("shift", [P, P])
        wrap = sb("wrap", [P, P])
        ones_row = sb("ones_row", [1, P])
        eps = sb("eps", [P, 1])
        wraw = sb("wraw", [P, 5, F])
        wt = sb("wt", [P, 5, F])
        brow = sb("brow", [1, 4, F])
        pool_bias = sb("pool_bias", [P, F])

        idx_win = sb("idx_win", [P, SLOTS, GC], U32)
        got = sb("got", [P, SLOTS, GC, F])
        mask = sb("mask", [P, SLOTS, GE], BF16)
        scan = sb("scan", [P, 2, GE])
        rows = sb("rows", [P, SLOTS, GC, F])

        node_win = sb("node_win", [P, TG], U32)
        node_got = sb("node_got", [P, TG, F])
        agg = sb("agg", [P, TG, F])
        agg_t = sb("agg_t", [P, TG, F])
        res = sb("res", [P, TG, F])
        xt = sb("xt", [P, TG, F])
        tab = sb("tab", [P, TG, F])
        stats = sb("stats", [P, TG, 6])
        mv = sb("mv", [P, TG, 2])
        sd = sb("sd", [P, TG])
        rstd = sb("rstd", [P, TG])

        bank_a = ps("bank_a", [P, 2, 512])
        bank_b = ps("bank_b", [P, 2, 512])
        bank_c = ps("bank_c", [P, 2, 512])
        bank_d = ps("bank_d", [P, 2, 512])

        def tiles(bank):
            return bank[:, :, :].rearrange("p a b -> p (a b)")[:, 0:TG * F].rearrange("p (t f) -> p t f", t=TG)

        na, nb, ncc, nd = tiles(bank_a), tiles(bank_b), tiles(bank_c), tiles(bank_d)

        edge_clear = sem("edge_clear")
        dst_loaded = sem("dst_loaded")
        prev_loaded = sem("prev_loaded")
        src_loaded = sem("src_loaded")
        wgt_loaded = sem("wgt_loaded")
        heads_loaded = sem("heads_loaded")
        par_loaded = sem("par_loaded")
        x_loaded = sem("x_loaded")
        x_clear = sem("x_clear")
        ids_made = sem("ids_made")
        const_made = sem("const_made")
        dst_cast = sem("dst_cast")
        masks_made = sem("masks_made")
        dst_stored = sem("dst_stored")
        masks_stored = sem("masks_stored")
        heads_cast = sem("heads_cast")
        heads_spread = sem("heads_spread")
        idh_made = sem("idh_made")
        counted = sem("counted")
        rows_found = sem("rows_found")
        level_got = [sem(f"level_got{k}") for k in range(4)]
        level_done = sem("level_done")
        count_done = sem("count_done")
        shifted = sem("shifted")
        deg_step = sem("deg_step")
        deg_done = sem("deg_done")
        root_done = sem("root_done")
        dinv_done = sem("dinv_done")
        z_made = sem("z_made")
        z_stored = sem("z_stored")
        self_made = sem("self_made")
        src_cast = sem("src_cast")
        flipped = sem("flipped")
        flip_copied = sem("flip_copied")
        src_wrapped = sem("src_wrapped")
        bias_spread = sem("bias_spread")
        bias_kept = sem("bias_kept")

        passed = {mybir.EngineType.Pool: sem("pool_passed"), mybir.EngineType.DVE: sem("dve_passed")}
        win_ready = sem("win_ready")
        gathered = [sem(f"gathered{s}") for s in range(SLOTS)]
        scaled = sem("scaled")
        turned = sem("turned")
        mask_here = [sem(f"mask_here{s}") for s in range(SLOTS)]
        scanned = sem("scanned")
        turned_back = sem("turned_back")
        rows_ready = sem("rows_ready")
        stored = [sem(f"stored{s}") for s in range(SLOTS)]

        node_win_ready = sem("node_win_ready")
        node_gathered = [sem(f"node_gathered{j}") for j in range(TG)]
        agg_made = sem("agg_made")
        agg_pre = sem("agg_pre")
        agg_turned = sem("agg_turned")
        agg_t_copied = sem("agg_t_copied")
        linear_done = sem("linear_done")
        res_made = sem("res_made")
        res_pre = sem("res_pre")
        stats_made = sem("stats_made")
        mv_made = sem("mv_made")
        sd_made = sem("sd_made")
        rstd_made = sem("rstd_made")
        normed = sem("normed")
        x1_kept = sem("x1_kept")
        x1_turned = sem("x1_turned")
        x1_t_copied = sem("x1_t_copied")
        heads_out = sem("heads_out")
        tab_ready = sem("tab_ready")
        half_kept = sem("half_kept")
        tab_stored = sem("tab_stored")
        self2_made = sem("self2_made")

        def wait(eng, s, n):
            if not isinstance(n, int) or n > 0:
                eng.wait_ge(s, n)

        def wait_alone(eng, s, n):
            wait(eng, s, n)
            eng.sem_inc(passed[eng.engine], 1)

        def turns(eng, n, body):
            body(0, True, False)
            with eng.Fori(1, n - 1) as i:
                body(i, False, False)
            body(n - 1, False, True)

        def blocks_to(dram, tile):
            return ((dram[0:(BLOCKS - 1) * P, :].rearrange("(b p) j -> p b j", p=P), tile[:, 0:BLOCKS - 1, :]),
                    (dram[(BLOCKS - 1) * P:CHUNKS, :], tile[0:LASTP, BLOCKS - 1, :]))

        def load_edges(sp, arr, tile, done):
            sp.dma_start(tile[:, 0:BLOCKS - 1, :],
                         arr[0:FULL].rearrange("(b p j) -> p b j", p=P, j=P)).then_inc(done, 16)
            sp.dma_start(tile[0:ROWS_LEFT, BLOCKS - 1, :],
                         arr[FULL:FULL + ROWS_LEFT * P].rearrange("(p j) -> p j", j=P)).then_inc(done, 16)
            sp.dma_start(tile[ROWS_LEFT:ROWS_LEFT + 1, BLOCKS - 1, 0:EDGES_LEFT],
                         arr[FULL + ROWS_LEFT * P:EDGES].rearrange("(p j) -> p j", p=1)).then_inc(done, 16)

        block = ctx.enter_context(nc.Block())

        @block.sync
        def _(sp):
            with nc.allow_non_contiguous_dma(reason="one destination per group, 403 in all"):
                sp.dma_start(heads_i[0:1, :], dst[0:(HEADS - 1) * GE + 1:GE].rearrange("(a n) -> a n", a=1))\
                  .then_inc(heads_loaded, 16)
            sp.wait_ge(edge_clear, 1)
            load_edges(sp, dst, dst_i, dst_loaded)
            load_edges(sp, src, src_i, src_loaded)
            sp.wait_ge(dst_cast, 1)
            flat = dst_rows.rearrange("g e -> (g e)").rearrange("(c j) -> c j", j=P)
            for dram, tile in blocks_to(flat, dst_f):
                sp.dma_start(dram, tile).then_inc(dst_stored, 16)
            load_edges(sp, edge_weight, wgt_f, wgt_loaded)
            sp.wait_ge(x_clear, 1)
            sp.dma_start(xin[:, 0:TILES - 1, :],
                         x[0:(TILES - 1) * P, :].rearrange("(t p) f -> p t f", p=P)).then_inc(x_loaded, 16)
            sp.dma_start(xin[0:TAIL, TILES - 1, :], x[(TILES - 1) * P:NODES, :]).then_inc(x_loaded, 16)
            sp.dma_start(prev_i[0:1, 0, 1:P], dst[0:P - 1].rearrange("(p j) -> p j", p=1)).then_inc(prev_loaded, 16)
            sp.dma_start(prev_i[1:P, 0, :], dst[P - 1:P * P - 1].rearrange("(p j) -> p j", j=P))\
              .then_inc(prev_loaded, 16)
            sp.dma_start(prev_i[:, 1:BLOCKS - 1, :],
                         dst[P * P - 1:FULL - 1].rearrange("(b p j) -> p b j", p=P, j=P)).then_inc(prev_loaded, 16)
            sp.dma_start(prev_i[0:ROWS_LEFT, BLOCKS - 1, :],
                         dst[FULL - 1:FULL + ROWS_LEFT * P - 1].rearrange("(p j) -> p j", j=P))\
              .then_inc(prev_loaded, 16)
            sp.dma_start(prev_i[ROWS_LEFT:ROWS_LEFT + 1, BLOCKS - 1, 0:EDGES_LEFT],
                         dst[FULL + ROWS_LEFT * P - 1:EDGES - 1].rearrange("(p j) -> p j", p=1))\
              .then_inc(prev_loaded, 16)
            for k, w in enumerate((w1, w2, pool_w, final_w[:, 0:F], final_w[:, F:2 * F])):
                sp.dma_start(wraw[:, k, :], w).then_inc(par_loaded, 16)
            for k, b in enumerate((b1, b2, final_b, pool_b)):
                sp.dma_start(brow[0:1, k, :], b.rearrange("(a f) -> a f", a=1)).then_inc(par_loaded, 16)
            sp.wait_ge(masks_made, 2)
            for dram, tile in ((sum_mask, smask), (max_mask, mmask)):
                for d, t in blocks_to(dram, tile):
                    sp.dma_start(d, t).then_inc(masks_stored, 16)
            sp.wait_ge(z_made, TILES)
            sp.dma_start(table[0].rearrange("(t p) f -> p t f", p=P), self1[:, :, :]).then_inc(z_stored, 16)
            sp.wait_ge(masks_stored, 64)

            for k in range(3):
                m = (sum_mask, sum_mask, max_mask)[k].rearrange("c j -> (c j)").rearrange("(a e) -> a e", a=1)
                done = k * GROUPS
                out_rows = scan_rows[k].rearrange("(c p) f -> p c f", p=P)

                def load_mask(g, s):
                    sp.dma_start(mask[:, s, :], m[0:1, bass.ds(g * GE, GE)].to_broadcast([P, GE]))\
                      .then_inc(mask_here[s], 16)

                wait(sp, scanned, done)
                for s in range(SLOTS - 1):
                    load_mask(s, s)

                def body(i, first, last):
                    for s in range(SLOTS):
                        g = i * SLOTS + s
                        if not (last and s > 0):
                            wait(sp, scanned, g + done)
                            load_mask(g + SLOTS - 1, (s + SLOTS - 1) % SLOTS)
                        sp.wait_ge(rows_ready, g + done + 1)
                        sp.dma_start(out_rows[:, bass.ds(g * GC, GC), :], rows[:, s, :, :]).then_inc(stored[s], 16)

                turns(sp, ROUNDS, body)

                def node(i, first, last):
                    sp.wait_ge(tab_ready, i + k * TURNS + 1)
                    if k < 2:
                        sp.dma_start(table[k + 1].rearrange("(t p) f -> p t f", p=P)[:, bass.ds(i * TG, TG), :],
                                     tab[:, :, :]).then_inc(tab_stored, 16)
                    elif not last:
                        sp.dma_start(out[0:(TILES - 1) * P, :].rearrange("(t p) f -> p t f", p=P)
                                     [:, bass.ds(i * TG, TG), :], tab[:, :, :]).then_inc(tab_stored, 16)
                    else:
                        sp.dma_start(out[i * TG * P:(TILES - 1) * P, :].rearrange("(t p) f -> p t f", p=P),
                                     tab[:, 0:TG - 1, :]).then_inc(tab_stored, 16)
                        sp.dma_start(out[(TILES - 1) * P:NODES, :], tab[0:TAIL, TG - 1, :])\
                          .then_inc(tab_stored, 16)

                turns(sp, TURNS, node)
            sp.wait_ge(tab_stored, 16 * (3 * TURNS + 1))

        @block.gpsimd
        def _(pool):
            nc.gpsimd.iota(ids_i[:, :], pattern=[[P, TILES]], base=0, channel_multiplier=1).then_inc(ids_made, 1)
            nc.gpsimd.memset(dst_i[:, BLOCKS - 1, :], int(NOWHERE))
            nc.gpsimd.memset(prev_i[:, 0, :], -1)
            nc.gpsimd.memset(prev_i[:, BLOCKS - 1, :], -1)
            nc.gpsimd.memset(src_i[:, BLOCKS - 1, :], 0)
            nc.gpsimd.memset(wgt_f[:, BLOCKS - 1, :], 0.0).then_inc(edge_clear, 1)
            nc.gpsimd.memset(xin[:, TILES - 1, :], 0.0).then_inc(x_clear, 1)
            for t, base in ((ident, 0), (shift, 1), (wrap, 1 - P)):
                nc.gpsimd.memset(t[:, :], 0.0).then_inc(const_made, 1)
            pool.wait_ge(const_made, 3)
            for t, base in ((ident, 0), (shift, 1), (wrap, 1 - P)):
                nc.gpsimd.affine_select(out=t[:, :], in_=t[:, :], compare_op=ALU.not_equal, fill=1.0, base=base,
                                        pattern=[[-1, P]], channel_multiplier=1).then_inc(const_made, 1)
            nc.gpsimd.memset(ones_row[:, :], 1.0).then_inc(const_made, 1)
            nc.gpsimd.memset(eps[:, :], EPS).then_inc(const_made, 1)

            pool.wait_ge(dst_stored, 32)
            for t in range(TILES):
                pool.wait_ge(rows_found, t + 1)
                if t >= 4:
                    pool.wait_ge(level_done, t - 3)
                nc.gpsimd.indirect_dma_start(level[:, t % 4, :], None, dst_rows[:, :],
                                             bass.IndirectOffsetOnAxis(ap=head_idx[:, t:t + 1], axis=0))\
                  .then_inc(level_got[t % 4], 16)

            for k in range(3):
                done = k * GROUPS
                if k == 0:
                    pool.wait_ge(z_stored, 16)
                else:
                    pool.wait_ge(tab_stored, 16 * k * TURNS)

                def body(i, first, last):
                    for s in range(SLOTS):
                        g = i * SLOTS + s
                        pool.wait_ge(win_ready, g + done + 1)
                        wait_alone(pool, turned, g + done - SLOTS + 1)
                        for c in range(GC):
                            nc.gpsimd.indirect_dma_start(
                                got[:, s, c, :], None, table[k][:, :],
                                bass.IndirectOffsetOnAxis(ap=idx_win[:, s, c:c + 1], axis=0))\
                              .then_inc(gathered[s], 16)

                turns(pool, ROUNDS, body)
                for s in range(SLOTS):
                    pool.wait_ge(stored[s], 16 * ROUNDS * (k + 1))

                def node(i, first, last):
                    for j in range(TG):
                        t = i * TG + j
                        pool.wait_ge(node_win_ready, t + k * TILES + 1)
                        wait_alone(pool, agg_made, t + k * TILES - TG + 1)
                        nc.gpsimd.indirect_dma_start(
                            node_got[:, j, :], None, scan_rows[k][:, :],
                            bass.IndirectOffsetOnAxis(ap=node_win[:, j:j + 1], axis=0))\
                          .then_inc(node_gathered[j], 16)

                turns(pool, TURNS, node)

        @block.scalar
        def _(act):
            act.wait_ge(heads_spread, 1)
            act.wait_ge(idh_made, 1)
            for t in range(TILES):
                if t >= 2:
                    act.wait_ge(counted, t - 1)
                nc.scalar.activation(sign_junk[:, t % 2, :], bank_d[:, 0, 0:HEADS], ACT.Sign, scale=-1.0,
                                     bias=idh[:, t:t + 1], accum_out=signs[:, t:t + 1]).then_inc(counted, 1)
            act.wait_ge(deg_done, 1)
            nc.scalar.activation(sdeg[:, :], deg[:, :], ACT.Sqrt).then_inc(root_done, 1)
            act.wait_ge(dinv_done, 1)
            act.wait_ge(x_loaded, 32)
            for t in range(0, TILES, 2):
                nc.scalar.activation(self1[:, t, :], xin[:, t, :], ACT.Copy, scale=dinv[:, t:t + 1])\
                  .then_inc(z_made, 1)
            act.wait_ge(z_stored, 16)
            act.wait_ge(z_made, TILES)
            for t in range(TILES):
                nc.scalar.activation(self1[:, t, :], self1[:, t, :], ACT.Copy, scale=dinv[:, t:t + 1])\
                  .then_inc(self_made, 1)

            for k in range(3):
                done = k * GROUPS

                def body(i, first, last):
                    for s in range(SLOTS):
                        g = i * SLOTS + s
                        if k == 2:
                            act.wait_ge(gathered[s], (i + k * ROUNDS + 1) * 16 * GC)
                            for c in range(GC):
                                a = nc.scalar.activation(got[:, s, c, :], got[:, s, c, :], ACT.Copy,
                                                         scale=wgt_t[:, bass.ds(g * GC + c, 1)])
                            a.then_inc(scaled, 1)
                        if s > 0 or not first:
                            b = (s - 1) % SLOTS
                            act.wait_ge(turned_back, g + done)
                            uses = i + k * ROUNDS - (1 if s == 0 else 0)
                            wait(act, stored[b], uses * 16)
                            nc.scalar.copy(rows[:, b, :, :], bank_b[:, b % 2, :]
                                           .rearrange("p (c f) -> p c f", c=GC)).then_inc(rows_ready, 1)

                turns(act, ROUNDS, body)
                b = SLOTS - 1
                act.wait_ge(turned_back, GROUPS + done)
                act.wait_ge(stored[b], 16 * ((k + 1) * ROUNDS - 1))
                nc.scalar.copy(rows[:, b, :, :], bank_b[:, b % 2, :].rearrange("p (c f) -> p c f", c=GC))\
                   .then_inc(rows_ready, 1)

                def node(i, first, last):
                    n = i + k * TURNS
                    act.wait_ge(agg_turned, n + 1)
                    nc.scalar.copy(agg_t[:, :, :], na).then_inc(agg_t_copied, 1)
                    if k == 0:
                        act.wait_ge(tab_ready, n + 1)
                        for j in range(TG):
                            a = nc.scalar.activation(self2[:, bass.ds(i * TG + j, 1), :].rearrange("p a f -> p (a f)"),
                                                     tab[:, j, :], ACT.Copy, scale=dinv[:, bass.ds(i * TG + j, 1)])
                        a.then_inc(self2_made, 1)
                    if k > 0:
                        act.wait_ge(mv_made, (i + (k - 1) * TURNS + 1) * TG)
                        nc.scalar.activation(sd[:, :], mv[:, :, 1], ACT.Sqrt, bias=eps[:, 0:1]).then_inc(sd_made, 1)
                    if k == 1:
                        act.wait_ge(x1_turned, i + 1)
                        nc.scalar.copy(xt[:, :, :], na).then_inc(x1_t_copied, 1)
                        act.wait_ge(heads_out, i + 1)
                        wait(act, tab_stored, 16 * n)
                        nc.scalar.copy(tab[:, :, :], ncc).then_inc(tab_ready, 1)

                turns(act, TURNS, node)

        @block.tensor
        def _(pe):
            pe.wait_ge(const_made, 8)
            pe.wait_ge(heads_cast, 1)
            nc.tensor.matmul(bank_d[:, 0, 0:HEADS], ones_row[:, :], heads_f[:, :], start=True, stop=True)\
              .then_inc(heads_spread, 1)
            jobs = [(src_f, b) for b in range(BLOCKS)] + [(wgt_f, b) for b in range(BLOCKS)] + \
                   [(wraw, b) for b in range(5)]

            def flip(n):
                t, b = jobs[n]
                if n >= 2:
                    pe.wait_ge(flip_copied, n - 1)
                h = LASTP if t is not wraw and b == BLOCKS - 1 else P
                nc.tensor.transpose(bank_a[:, n % 2, 0:h], t[0:h, b, :], ident[0:h, 0:h]).then_inc(flipped, 1)

            pe.wait_ge(src_cast, 1)
            for n in range(BLOCKS):
                flip(n)
            pe.wait_ge(count_done, TILES + 1)
            nc.tensor.matmul(bank_b[:, 0, 0:TILES], shift[:, :], count[:, 1:TILES + 1], start=True, stop=False)
            nc.tensor.matmul(bank_b[:, 0, 0:TILES], wrap[:, :], count[:, 0:TILES], start=False, stop=True)\
              .then_inc(shifted, 1)
            pe.wait_ge(wgt_loaded, 48)
            pe.wait_ge(par_loaded, 9 * 16)
            for n in range(BLOCKS, len(jobs)):
                flip(n)
            nc.tensor.matmul(bank_c[:, 0, 0:F], ones_row[:, :], brow[0:1, 3, :], start=True, stop=True)\
              .then_inc(bias_spread, 1)
            pe.wait_ge(deg_done, 1)
            pe.wait_ge(flip_copied, len(jobs))

            for k in range(3):
                done = k * GROUPS

                def body(i, first, last):
                    for s in range(SLOTS):
                        g = i * SLOTS + s
                        if k == 2:
                            pe.wait_ge(scaled, g + 1)
                        else:
                            pe.wait_ge(gathered[s], (i + k * ROUNDS + 1) * 16 * GC)
                        wait(pe, scanned, g + done - 1)
                        for c in range(GC):
                            a = nc.tensor.transpose(bank_a[:, s % 2, c * P:(c + 1) * P], got[:, s, c, :], ident[:, :])
                        a.then_inc(turned, 1)
                        if s > 0 or not first:
                            back(g - 1 + done, (s - 1) % 2)

                def back(n, q):
                    pe.wait_ge(scanned, n + 1)
                    wait(pe, rows_ready, n - 1)
                    for c in range(GC):
                        a = nc.tensor.transpose(bank_b[:, q, c * P:(c + 1) * P], scan[:, q, c * P:(c + 1) * P],
                                                ident[:, :])
                    a.then_inc(turned_back, 1)

                turns(pe, ROUNDS, body)
                back(GROUPS - 1 + done, (SLOTS - 1) % 2)
                pe.wait_ge(rows_ready, GROUPS + done)

                def node(i, first, last):
                    n = i + k * TURNS
                    pe.wait_ge(agg_made, (n + 1) * TG)
                    wait(pe, agg_t_copied, n)
                    if k == 1:
                        wait(pe, x1_t_copied, i)
                    for j in range(TG):
                        a = nc.tensor.transpose(na[:, j, :], agg[:, j, :], ident[:, :])
                    a.then_inc(agg_turned, 1)
                    pe.wait_ge(agg_t_copied, n + 1)
                    if k == 0:
                        wait(pe, tab_ready, n)
                    else:
                        wait(pe, res_made, n - TURNS)
                    for j in range(TG):
                        a = nc.tensor.matmul(nb[:, j, :], agg_t[:, j, :], wt[:, (0, 1, 4)[k], :],
                                             start=True, stop=(k == 2))
                        if k < 2:
                            a = nc.tensor.matmul(nb[:, j, :], ones_row[:, :], brow[0:1, k, :], start=False, stop=True)
                    a.then_inc(linear_done, 1)
                    if k == 1:
                        pe.wait_ge(normed, i + 1)
                        for j in range(TG):
                            a = nc.tensor.transpose(na[:, j, :], res[:, j, :], ident[:, :])
                        a.then_inc(x1_turned, 1)
                        pe.wait_ge(x1_t_copied, i + 1)
                        wait(pe, tab_ready, n)
                        wait(pe, half_kept, i)
                        for j in range(TG):
                            nc.tensor.matmul(ncc[:, j, :], xt[:, j, :], wt[:, 2, :], start=True, stop=True)
                            nc.tensor.matmul(nd[:, j, :], xt[:, j, :], wt[:, 3, :], start=True, stop=False)
                            a = nc.tensor.matmul(nd[:, j, :], ones_row[:, :], brow[0:1, 2, :], start=False, stop=True)
                        a.then_inc(heads_out, 1)

                turns(pe, TURNS, node)

        @block.vector
        def _(dve):
            dve.wait_ge(heads_loaded, 16)
            nc.vector.tensor_copy(heads_f[:, :], heads_i[:, :]).then_inc(heads_cast, 1)
            dve.wait_ge(ids_made, 1)
            nc.vector.tensor_copy(ids[:, :], ids_i[:, :]).then_inc(ids_made, 1)
            dve.wait_ge(ids_made, 2)
            nc.vector.tensor_scalar(idh[:, :], ids[:, :], 0.5, None, ALU.add).then_inc(idh_made, 1)
            nc.vector.memset(count[:, 0:1], 0.0).then_inc(count_done, 1)
            dve.wait_ge(dst_loaded, 48)
            nc.vector.tensor_copy(dst_f[:, :, :], dst_i[:, :, :]).then_inc(dst_cast, 1)

            def take(n):
                dve.wait_ge(flipped, n + 1)
                kind, b = (0, n) if n < BLOCKS else (1, n - BLOCKS) if n < 2 * BLOCKS else (2, n - 2 * BLOCKS)
                h = LASTP if kind < 2 and b == BLOCKS - 1 else P
                to = wt[:, b, :] if kind == 2 else (src_t, wgt_t)[kind][:, b * P:b * P + h]
                nc.vector.tensor_copy(to, bank_a[:, n % 2, 0:h]).then_inc(flip_copied, 1)

            dve.wait_ge(src_loaded, 48)
            nc.vector.tensor_copy(src_f[:, :, :], src_i[:, :, :]).then_inc(src_cast, 1)
            for n in range(BLOCKS):
                take(n)
            dve.wait_ge(flip_copied, BLOCKS)
            nc.vector.tensor_copy(src_t[:, CHUNKS:CHUNKS + SLOTS * GC], src_t[:, 0:SLOTS * GC]).then_inc(src_wrapped, 1)
            for s in range(SLOTS):
                nc.vector.tensor_copy(idx_win[:, s, :], src_t[:, s * GC:(s + 1) * GC]).then_inc(win_ready, 1)

            def find_row(t):
                dve.wait_ge(counted, t + 1)
                nc.vector.tensor_scalar(head_row[:, t:t + 1], signs[:, t:t + 1], 0.5, HEADS / 2 - 1.0,
                                        ALU.mult, ALU.add).then_inc(deg_step, 1)
                dve.wait_ge(deg_step, 2 * t + 1)
                nc.vector.tensor_scalar(head_row[:, t:t + 1], head_row[:, t:t + 1], 0.0, None, ALU.max)\
                   .then_inc(deg_step, 1)
                dve.wait_ge(deg_step, 2 * t + 2)
                nc.vector.tensor_copy(head_idx[:, t:t + 1], head_row[:, t:t + 1]).then_inc(rows_found, 1)

            def count_row(t):
                dve.wait_ge(level_got[t % 4], 16 * (t // 4 + 1))
                nc.vector.tensor_scalar(level_junk[:, :], level[:, t % 4, :], ids[:, t:t + 1], None, ALU.is_le,
                                        ALU.add, accum_out=inner[:, t:t + 1]).then_inc(level_done, 1)
                dve.wait_ge(level_done, t + 1)
                nc.vector.scalar_tensor_tensor(out=count[:, t + 1:t + 2], in0=head_row[:, t:t + 1], scalar=float(GE),
                                               in1=inner[:, t:t + 1], op0=ALU.mult, op1=ALU.add)\
                   .then_inc(count_done, 1)

            LAG = 4
            for t in range(TILES + LAG):
                if t < TILES:
                    find_row(t)
                if t >= LAG:
                    count_row(t - LAG)
            dve.wait_ge(shifted, 1)
            dve.wait_ge(count_done, TILES + 1)
            nc.vector.tensor_tensor(indeg[:, :], count[:, 1:TILES + 1], bank_b[:, 0, 0:TILES], ALU.subtract)\
              .then_inc(deg_step, 1)
            n = 2 * TILES + 1
            dve.wait_ge(deg_step, n)
            nc.vector.tensor_scalar(deg[:, :], indeg[:, :], 1.0, None, ALU.add).then_inc(deg_done, 1)
            nc.vector.tensor_scalar(has[:, :], indeg[:, :], 1.0, None, ALU.min)
            nc.vector.tensor_scalar(last_f[:, :], count[:, 1:TILES + 1], -1.0, 0.0, ALU.add, ALU.max)\
              .then_inc(deg_step, 1)
            dve.wait_ge(deg_step, n + 1)
            nc.vector.tensor_copy(last_idx[:, 0:TILES], last_f[:, :])
            nc.vector.tensor_copy(last_idx[:, TILES:TILES + TG], last_f[:, 0:TG]).then_inc(deg_step, 1)
            dve.wait_ge(root_done, 1)
            nc.vector.reciprocal(dinv[:, :], sdeg[:, :]).then_inc(dinv_done, 1)
            dve.wait_ge(dinv_done, 1)
            nc.vector.tensor_tensor(dinv_has[:, :], dinv[:, :], has[:, :], ALU.mult).then_inc(deg_step, 1)
            dve.wait_ge(x_loaded, 32)
            for t in range(1, TILES, 2):
                nc.vector.tensor_scalar(self1[:, t, :], xin[:, t, :], dinv[:, t:t + 1], None, ALU.mult)\
                   .then_inc(z_made, 1)
            dve.wait_ge(deg_step, n + 3)
            nc.vector.tensor_copy(node_win[:, :], last_idx[:, 0:TG]).then_inc(node_win_ready, TG)

            for n in range(BLOCKS, 2 * BLOCKS + 5):
                take(n)
            dve.wait_ge(bias_spread, 1)
            nc.vector.tensor_copy(pool_bias[:, :], bank_c[:, 0, 0:F]).then_inc(bias_kept, 1)
            dve.wait_ge(prev_loaded, 80)
            nc.vector.tensor_tensor(smask[:, :, :], dst_i[:, :, :], prev_i[:, :, :], ALU.is_equal)\
              .then_inc(masks_made, 1)
            dve.wait_ge(masks_made, 1)
            nc.vector.tensor_scalar(mmask[:, :, :], smask[:, :, :], 1.0, -RESET, ALU.subtract, ALU.mult)\
              .then_inc(masks_made, 1)
            dve.wait_ge(flip_copied, 2 * BLOCKS + 5)
            dve.wait_ge(src_wrapped, 1)
            dve.wait_ge(bias_kept, 1)

            for k in range(3):
                done = k * GROUPS
                op0, op1 = (ALU.mult, ALU.add) if k < 2 else (ALU.add, ALU.max)

                def body(i, first, last):
                    for s in range(SLOTS):
                        g = i * SLOTS + s
                        wait_alone(dve, gathered[s], (i + k * ROUNDS + 1) * 16 * GC)
                        nc.vector.tensor_copy(idx_win[:, s, :], src_t[:, bass.ds((g + SLOTS) * GC, GC)])\
                           .then_inc(win_ready, 1)
                        dve.wait_ge(turned, g + done + 1)
                        dve.wait_ge(mask_here[s], (i + k * ROUNDS + 1) * 16)
                        wait(dve, turned_back, g + done - 1)
                        wait(dve, scanned, g + done)
                        init = 0.0 if first and s == 0 else scan[:, (s - 1) % 2, GE - 1:GE]
                        nc.vector.tensor_tensor_scan(scan[:, s % 2, :], mask[:, s, :], bank_a[:, s % 2, :],
                                                     init, op0, op1).then_inc(scanned, 1)

                turns(dve, ROUNDS, body)

                def node(i, first, last):
                    n = i + k * TURNS
                    for j in range(TG):
                        t = i * TG + j
                        dve.wait_ge(node_gathered[j], (n + 1) * 16)
                        wait(dve, agg_turned, n)
                        row = node_got[:, j, :]
                        if k < 2:
                            own = (self1, self2)[k][:, bass.ds(t, 1), :].rearrange("p a f -> p (a f)")
                            if first and j == 0:
                                dve.wait_ge(self_made, TILES) if k == 0 else dve.wait_ge(self2_made, TURNS)
                            nc.vector.scalar_tensor_tensor(out=agg[:, j, :], in0=row,
                                                           scalar=dinv_has[:, bass.ds(t, 1)], in1=own,
                                                           op0=ALU.mult, op1=ALU.add).then_inc(agg_made, 1)
                        else:
                            nc.vector.tensor_tensor(agg[:, j, :], row, pool_bias[:, :], ALU.add).then_inc(agg_pre, 1)
                            dve.wait_ge(agg_pre, t + 1)
                            nc.vector.tensor_scalar(agg[:, j, :], agg[:, j, :], 0.0, has[:, bass.ds(t, 1)],
                                                    ALU.max, ALU.mult).then_inc(agg_made, 1)
                        nc.vector.tensor_copy(node_win[:, j:j + 1], last_idx[:, bass.ds(t + TG, 1)] if not last
                                              else last_idx[:, j:j + 1]).then_inc(node_win_ready, 1)
                    dve.wait_ge(linear_done, n + 1)
                    if k == 0:
                        wait(dve, tab_stored, n * 16)
                        wait(dve, self2_made, i)
                        for j in range(TG):
                            t = i * TG + j
                            a = nc.vector.tensor_scalar(tab[:, j, :], nb[:, j, :], 0.0, dinv[:, bass.ds(t, 1)],
                                                        ALU.max, ALU.mult)
                        a.then_inc(tab_ready, 1)
                        return
                    if k == 1:
                        wait(dve, x1_turned, i)
                    old = xin[:, bass.ds(i * TG, TG), :]
                    if k == 2 and first:
                        dve.wait_ge(x1_kept, TURNS)
                        dve.wait_ge(half_kept, TURNS)
                    if k == 1:
                        nc.vector.tensor_tensor(res[:, :, :], nb, old, ALU.add).then_inc(res_made, 1)
                    else:
                        nc.vector.tensor_tensor(res[:, :, :], nb, self2[:, bass.ds(i * TG, TG), :], ALU.add)\
                           .then_inc(res_pre, 1)
                        dve.wait_ge(res_pre, i + 1)
                        nc.vector.scalar_tensor_tensor(out=res[:, :, :], in0=res[:, :, :], scalar=0.0, in1=old,
                                                       op0=ALU.max, op1=ALU.add).then_inc(res_made, 1)
                    m = i + (k - 1) * TURNS
                    dve.wait_ge(res_made, m + 1)
                    for j in range(TG):
                        nc.vector.bn_stats(stats[:, j, :], res[:, j, :]).then_inc(stats_made, 1)
                    wait_alone(dve, stats_made, m * TG + TG)
                    for j in range(TG):
                        nc.vector.bn_aggr(mv[:, j, :], stats[:, j, :]).then_inc(mv_made, 1)
                    dve.wait_ge(sd_made, m + 1)
                    nc.vector.reciprocal(rstd[:, :], sd[:, :]).then_inc(rstd_made, 1)
                    dve.wait_ge(rstd_made, m + 1)
                    if k == 2:
                        wait(dve, tab_stored, n * 16)
                    for j in range(TG):
                        to = res[:, j, :] if k == 1 else tab[:, j, :]
                        a = nc.vector.tensor_scalar(to, res[:, j, :], mv[:, j, 0:1], rstd[:, j:j + 1],
                                                    ALU.subtract, ALU.mult)
                    a.then_inc(normed if k == 1 else tab_ready, 1)
                    if k == 1:
                        wait_alone(dve, normed, i + 1)
                        nc.vector.tensor_copy(old, res[:, :, :]).then_inc(x1_kept, 1)
                        wait_alone(dve, heads_out, i + 1)
                        nc.vector.tensor_copy(self2[:, bass.ds(i * TG, TG), :], nd).then_inc(half_kept, 1)

                turns(dve, TURNS, node)


_INS = ["x", "src", "dst", "edge_weight", "L0_gnn_W1", "L0_gnn_b1", "L0_gnn_W2", "L0_gnn_b2",
        "L1_gnn_pool_w", "L1_gnn_pool_b", "L1_gnn_final_w", "L1_gnn_final_b"]


def kernel(**inputs):
    import numpy as _np
    import concourse.bacc as _bacc
    from concourse import mybir as _mybir
    from concourse.bass_utils import run_bass_kernel_spmd as _run

    nc = _bacc.Bacc("TRN2", target_bir_lowering=False, num_devices=1)
    arrays, args = {}, []
    for name in _INS:
        a = _np.ascontiguousarray(inputs[name])
        arrays[f"in_{name}"] = a
        args.append(nc.dram_tensor(f"in_{name}", a.shape, _mybir.dt.from_np(a.dtype), kind="ExternalInput").ap())
    result = nc.dram_tensor("out_0", (NODES, F), F32, kind="ExternalOutput").ap()
    program(nc, *args, result)
    r = _run(nc, [arrays], core_ids=[0])
    return r.results[0]["out_0"]
```

```python
from contextlib import ExitStack

import concourse.bass as bass
from concourse import mybir

P = 128
F = 128
NODES = 6250
EDGES = 206250
TILES = -(-NODES // P)
NPAD = TILES * P
TAIL = NODES - (TILES - 1) * P
GC = 4
GE = GC * P
SLOTS = 4
ROUNDS = -(-EDGES // (GE * SLOTS))
GROUPS = ROUNDS * SLOTS
WIN = 8
POOL_CH = 12
DENSE_CH = 16
TURN_CH = POOL_CH + DENSE_CH
CELL_BLOCKS = -(-TILES * WIN // P)
MID = TILES * WIN // 2
POOL_SL = POOL_CH // GC
FT = 2 * -(-EDGES // (P * TURN_CH * 2))
PC, DC = POOL_CH * WIN, DENSE_CH * WIN
TC = PC + DC
BLOCKS = -(-max(GROUPS * GC, FT * TURN_CH) // P)
CHUNKS = BLOCKS * P
FULL = (BLOCKS - 1) * P * P
ROWS_LEFT = (EDGES - FULL) // P
EDGES_LEFT = EDGES - FULL - ROWS_LEFT * P
HEADS = -(-EDGES // GE)
TG = 7
TURNS = TILES // TG
PRODUCTS_AT = (4, 8, 12)
RESET = -3.3e38
NOWHERE = 1.0e5
EPS = 1e-5

ALU = mybir.AluOpType
ACT = mybir.ActivationFunctionType
AX = mybir.AxisListType
F32 = mybir.dt.float32
BF16 = mybir.dt.bfloat16
I32 = mybir.dt.int32
I16 = mybir.dt.int16
U32 = mybir.dt.uint32


def program(nc, x, src, dst, edge_weight, w1, b1, w2, b2, pool_w, pool_b, final_w, final_b, out):
    with ExitStack() as ctx:
        def sb(name, shape, dt=F32):
            return ctx.enter_context(nc.sbuf_tensor(name, shape, dt))

        def ps(name, shape, dt=F32):
            return ctx.enter_context(nc.psum_tensor(name, shape, dt))

        def sem(name):
            return ctx.enter_context(nc.semaphore(name))

        table = [nc.dram_tensor(f"table{k}", [NPAD, F], F32, kind="Internal").ap() for k in range(3)]
        scan_rows = [nc.dram_tensor(f"scan_rows{k}", [GROUPS * GE, F], F32, kind="Internal").ap() for k in range(3)]
        col_rows = [nc.dram_tensor(f"col_rows{k}", [FT * TC, F], F32, kind="Internal").ap() for k in range(2)]
        dst_rows = nc.dram_tensor("dst_rows", [CHUNKS // GC, GE], F32, kind="Internal").ap()
        sum_mask = nc.dram_tensor("sum_mask", [CHUNKS, P], BF16, kind="Internal").ap()
        max_mask = nc.dram_tensor("max_mask", [CHUNKS, P], BF16, kind="Internal").ap()
        col_mask = nc.dram_tensor("col_mask", [CHUNKS, WIN], BF16, kind="Internal").ap()

        EB = BLOCKS * P
        words = 9 * EB + 4 * GE + GE + 2 * HEADS + 5 * F
        region = sb("region", [P, words])
        taken = [0]

        def part(shape, dt=F32):
            n = 1
            for d in shape[1:]:
                n *= d
            w = n * (2 if dt == BF16 else 4) // 4
            v = region[:, taken[0]:taken[0] + w]
            taken[0] += w
            v = v if dt == F32 else v.bitcast(dt)
            if len(shape) == 3:
                return v.rearrange("p (a b) -> p a b", b=shape[2])
            if len(shape) == 4:
                return v.rearrange("p (a b c) -> p a b c", b=shape[2], c=shape[3])
            return v

        src_i = part([P, BLOCKS, P], I32)
        dst_i = part([P, BLOCKS, P], I32)
        prev_i = part([P, BLOCKS, P], I32)
        src_f = part([P, BLOCKS, P])
        wgt_f = part([P, BLOCKS, P])
        dst_f = part([P, BLOCKS, P])
        off_f = part([P, BLOCKS, P])
        cell_f = part([P, BLOCKS, P])
        smask = part([P, BLOCKS, P], BF16)
        mmask = part([P, BLOCKS, P], BF16)
        level = part([P, 4, GE])
        level_junk = part([P, GE])
        sign_junk = part([P, 2, HEADS])
        wraw = part([P, 5, F])
        assert taken[0] <= words
        taken[0] = 0
        parts = part([P, 3, TILES, F], BF16)
        counts = part([P, 2, TILES, DC], BF16)
        rest = part([P, TG, F])
        hot_low = part([P, 4, P], BF16)
        hot_cell = part([P, 4, TILES * WIN], BF16)
        hot_off = part([P, 2, POOL_CH, WIN])
        col_m = part([P, 2, TC], BF16)
        xn = part([P, TG, F])
        stats = part([P, TG, 6])
        assert taken[0] <= words

        src_t = sb("src_t", [P, EB], U32)
        wgt_t = sb("wgt_t", [P, EB])
        off_t = sb("off_t", [P, EB], BF16)
        low_t = sb("low_t", [P, EB], BF16)
        cell_t = sb("cell_t", [P, EB], BF16)
        span = sb("span", [P, BLOCKS])
        spanm = sb("spanm", [P, 1])
        spanr = sb("spanr", [1, 1])
        short_f = sb("short_f", [1, 1])
        short_i = sb("short_i", [1, 1], I32)
        short_p = sb("short_p", [P, 1])
        cmask = sb("cmask", [P, BLOCKS, WIN], BF16)
        cell_no = sb("cell_no", [P, CELL_BLOCKS, P], BF16)
        ident_b = sb("ident_b", [P, P], BF16)
        iota_f = sb("iota_f", [P, WIN])

        xin = sb("xin", [P, TILES, F])
        own = sb("own", [P, TILES, F])
        ids_i = sb("ids_i", [P, TILES], I32)
        ids = sb("ids", [P, TILES])
        idh = sb("idh", [P, TILES])
        signs = sb("signs", [P, TILES])
        head_row = sb("head_row", [P, TILES])
        head_idx = sb("head_idx", [P, TILES], U32)
        inner = sb("inner", [P, TILES])
        count = sb("count", [P, TILES + 1])
        indeg = sb("indeg", [P, TILES])
        indeg_i = sb("indeg_i", [P, TILES], I32)
        indeg_r = sb("indeg_r", [P, TILES])
        deg = sb("deg", [P, TILES])
        sdeg = sb("sdeg", [P, TILES])
        dinv = sb("dinv", [P, TILES])
        has = sb("has", [P, TILES])
        h4 = sb("h4", [P, TILES, GC])
        le4 = sb("le4", [P, TILES, GC])
        nle = sb("nle", [P, TILES])
        first_dst = sb("first_dst", [P, TILES])
        pos = sb("pos", [P, TILES])
        posd = sb("posd", [P, TILES])
        last_f = sb("last_f", [P, TILES])
        last_idx = sb("last_idx", [P, 2, TILES + 2 * TG], U32)
        own_flat = own[:, :, :].rearrange("p t f -> p (t f)")
        cell_no_i = own_flat[:, 2 * HEADS + 2:2 * HEADS + 2 + CELL_BLOCKS * P // 2].bitcast(I16)
        iota_i = own_flat[:, 4 * F * CELL_BLOCKS:4 * F * CELL_BLOCKS + WIN].bitcast(I32)
        heads_f = own_flat[0:1, 0:HEADS]
        heads_i = own_flat[0:1, HEADS:2 * HEADS].bitcast(I32)

        ident = sb("ident", [P, P])
        shift = sb("shift", [P, P])
        wrap = sb("wrap", [P, P])
        ones_row = sb("ones_row", [1, P])
        eps = sb("eps", [P, 1])
        wt = sb("wt", [P, 5, F])
        brow = sb("brow", [1, 4, F])
        bias = sb("bias", [P, 4, F])

        idx_win = sb("idx_win", [P, SLOTS, GC], U32)
        idx_turn = sb("idx_turn", [P, 2, POOL_CH], U32)
        got = sb("got", [P, SLOTS, GC, F])
        mask = sb("mask", [P, SLOTS, GE], BF16)
        scan = sb("scan", [P, 2, GE])
        rows = sb("rows", [P, SLOTS, GC, F])

        node_win = sb("node_win", [P, 2, TG], U32)
        node_got = got[:, :, :, :].rearrange("p s c f -> p (s c) f")[:, 0:2 * TG, :]\
            .rearrange("p (h t) f -> p h t f", h=2)
        agg = sb("agg", [P, TG, F])
        agg_t = sb("agg_t", [P, TG, F])
        res = sb("res", [P, TG, F])
        tab = sb("tab", [P, TG, F])
        mv = sb("mv", [P, TG, 2])
        sd = sb("sd", [P, TG])
        rstd = sb("rstd", [P, TG])

        bank_a = ps("bank_a", [P, 2, 512])
        bank_b = ps("bank_b", [P, 2, 512])
        bank_c = ps("bank_c", [P, 2, 512])
        bank_d = ps("bank_d", [P, 2, 512])

        def tiles(bank):
            return bank[:, :, :].rearrange("p a b -> p (a b)")[:, 0:TG * F].rearrange("p (t f) -> p t f", t=TG)

        na, nb, ncc, nd = tiles(bank_a), tiles(bank_b), tiles(bank_c), tiles(bank_d)

        edge_clear = sem("edge_clear")
        dst_loaded = sem("dst_loaded")
        prev_loaded = sem("prev_loaded")
        src_loaded = sem("src_loaded")
        wgt_loaded = sem("wgt_loaded")
        heads_loaded = sem("heads_loaded")
        par_loaded = sem("par_loaded")
        x_loaded = sem("x_loaded")
        x_clear = sem("x_clear")
        ids_made = sem("ids_made")
        const_made = sem("const_made")
        dst_cast = sem("dst_cast")
        masks_made = sem("masks_made")
        dst_stored = sem("dst_stored")
        masks_stored = sem("masks_stored")
        heads_cast = sem("heads_cast")
        heads_spread = sem("heads_spread")
        idh_made = sem("idh_made")
        counted = sem("counted")
        rows_found = sem("rows_found")
        level_got = [sem(f"level_got{k}") for k in range(4)]
        level_done = sem("level_done")
        count_done = sem("count_done")
        shifted = sem("shifted")
        deg_step = sem("deg_step")
        deg_done = sem("deg_done")
        root_done = sem("root_done")
        dinv_done = sem("dinv_done")
        z_made = sem("z_made")
        z_stored = sem("z_stored")
        src_cast = sem("src_cast")
        flipped = sem("flipped")
        flip_copied = sem("flip_copied")
        src_wrapped = sem("src_wrapped")
        bias_spread = sem("bias_spread")
        bias_kept = sem("bias_kept")
        prep = sem("prep")
        cols_stored = sem("cols_stored")
        span_turned = sem("span_turned")
        short_spread = sem("short_spread")
        short_known = sem("short_known")
        iota_made = sem("iota_made")
        iota_spread = sem("iota_spread")
        idx_step = sem("idx_step")
        x_biased = sem("x_biased")
        own_done = sem("own_done")

        WINDOWS = TURNS + 2
        passed = {mybir.EngineType.Pool: sem("pool_passed"), mybir.EngineType.DVE: sem("dve_passed")}
        def sems(name, n):
            return [sem(f"{name}{k}") for k in range(n)]

        win_ready = sems("win_ready", 3)
        gathered = [sems(f"gathered{k}_", SLOTS) for k in range(3)]
        scaled = sem("scaled")
        turned = sems("turned", 3)
        mask_here = [sems(f"mask_here{k}_", SLOTS) for k in range(3)]
        scanned = sems("scanned", 3)
        turned_back = sems("turned_back", 3)
        rows_ready = sems("rows_ready", 3)
        stored = [sems(f"stored{k}_", SLOTS) for k in range(3)]
        hot_ready = sems("hot_ready", 2)
        off_ready = sems("off_ready", 2)
        built = sems("built", 2)
        kept = sems("kept", 2)
        applied = sems("applied", 2)
        part_hi = sems("part_hi", 2)
        rest_hi = sems("rest_hi", 2)
        part_mid = sems("part_mid", 2)
        parts_done = sems("parts_done", 2)

        node_win_ready = sem("node_win_ready")
        node_gathered = sems("node_gathered", 2)
        agg_made = sem("agg_made")
        agg_pre = sem("agg_pre")
        agg_turned = sem("agg_turned")
        agg_t_copied = sem("agg_t_copied")
        linear_done = sem("linear_done")
        res_made = sem("res_made")
        res_pre = sem("res_pre")
        stats_made = sem("stats_made")
        mv_made = sem("mv_made")
        sd_made = sem("sd_made")
        rstd_made = sem("rstd_made")
        normed = sem("normed")
        x1_kept = sem("x1_kept")
        x1_turned = sem("x1_turned")
        x1_t_copied = sem("x1_t_copied")
        heads_out = sem("heads_out")
        tab_ready = sem("tab_ready")
        half_kept = sem("half_kept")
        half_biased = sem("half_biased")
        tab_stored = sem("tab_stored")

        def wait(eng, s, n):
            if not isinstance(n, int) or n > 0:
                eng.wait_ge(s, n)

        def wait_alone(eng, s, n):
            wait(eng, s, n)
            eng.sem_inc(passed[eng.engine], 1)

        def turns(eng, n, body):
            body(0, True, False)
            with eng.Fori(1, n - 1) as i:
                body(i, False, False)
            body(n - 1, False, True)

        def turn_pairs(eng, body):
            body(0, 0, 0, True)
            body(1, 1, 0, True)
            body(2, 0, 1, False)
            body(3, 1, 1, False)
            with eng.Fori(2, FT // 2) as i:
                body(2 * i, 0, i, False)
                body(2 * i + 1, 1, i, False)

        def node_steps(eng, front, back):
            front(0, 0, 0)
            front(1, 1, 0)
            back(0, 0, 0)
            front(2, 0, 1)
            back(1, 1, 0)
            with eng.Fori(1, TURNS // 2) as m:
                front(2 * m + 1, 1, m)
                back(2 * m, 0, m)
                front(2 * m + 2, 0, m + 1)
                back(2 * m + 1, 1, m)
            back(TURNS - 1, 0, TURNS // 2)

        def ways(eng, k, short, general):
            if k == 2:
                general()
                return
            if k == 0:
                eng.wait_ge(short_known, 1)
            go = eng.value_load(short_i[0:1, 0:1], min_val=0, max_val=1)
            with eng.If(go == 1):
                short()
            with eng.Else():
                general()

        def blocks_of(dram, tile):
            return dram.rearrange("(b p) j -> p b j", p=P), tile

        def load_edges(sp, arr, tile, done):
            sp.dma_start(tile[:, 0:BLOCKS - 1, :],
                         arr[0:FULL].rearrange("(b p j) -> p b j", p=P, j=P)).then_inc(done, 16)
            sp.dma_start(tile[0:ROWS_LEFT, BLOCKS - 1, :],
                         arr[FULL:FULL + ROWS_LEFT * P].rearrange("(p j) -> p j", j=P)).then_inc(done, 16)
            sp.dma_start(tile[ROWS_LEFT:ROWS_LEFT + 1, BLOCKS - 1, 0:EDGES_LEFT],
                         arr[FULL + ROWS_LEFT * P:EDGES].rearrange("(p j) -> p j", p=1)).then_inc(done, 16)

        def one(tile, t):
            return tile[:, bass.ds(t, 1), :].rearrange("p a f -> p (a f)")

        flips = [(kind, t, b, to[:, b * P:(b + 1) * P])
                 for kind, t, to in (("src", src_f, src_t), ("off", off_f, off_t), ("low", src_f, low_t),
                                     ("cell", cell_f, cell_t), ("wgt", wgt_f, wgt_t)) for b in range(BLOCKS)]
        flips += [("par", wraw, b, wt[:, b, :]) for b in range(5)]
        SPAN_STEP, LOW_STEP, CELL_STEP, PREP = 4, 6, 9, 13
        FLIPPED = len(flips)
        flip_needs = {"src": (src_cast, 1), "off": (prep, 1), "low": (prep, LOW_STEP), "cell": (prep, CELL_STEP),
                      "wgt": (wgt_loaded, 48), "par": (par_loaded, 9 * 16)}
        build = [b[:, h, 0:TILES * WIN] for b, h in ((bank_c, 0), (bank_c, 1))]
        iota = bank_d[:, 0, :].bitcast(BF16)[:, 0:TILES * WIN]

        block = ctx.enter_context(nc.Block())

        @block.sync
        def _(sp):
            with nc.allow_non_contiguous_dma(reason="one destination per group, 403 in all"):
                sp.dma_start(heads_i[0:1, :], dst[0:(HEADS - 1) * GE + 1:GE].rearrange("(a n) -> a n", a=1))\
                  .then_inc(heads_loaded, 16)
            sp.wait_ge(edge_clear, 1)
            load_edges(sp, dst, dst_i, dst_loaded)
            load_edges(sp, src, src_i, src_loaded)
            sp.wait_ge(dst_cast, 1)
            flat = dst_rows.rearrange("g e -> (g e)").rearrange("(c j) -> c j", j=P)
            sp.dma_start(*blocks_of(flat, dst_f)).then_inc(dst_stored, 16)
            sp.dma_start(prev_i[0:1, 0, 1:P], dst[0:P - 1].rearrange("(p j) -> p j", p=1)).then_inc(prev_loaded, 16)
            sp.dma_start(prev_i[1:P, 0, :], dst[P - 1:P * P - 1].rearrange("(p j) -> p j", j=P))\
              .then_inc(prev_loaded, 16)
            sp.dma_start(prev_i[:, 1:BLOCKS - 1, :],
                         dst[P * P - 1:FULL - 1].rearrange("(b p j) -> p b j", p=P, j=P)).then_inc(prev_loaded, 16)
            sp.dma_start(prev_i[0:ROWS_LEFT, BLOCKS - 1, :],
                         dst[FULL - 1:FULL + ROWS_LEFT * P - 1].rearrange("(p j) -> p j", j=P))\
              .then_inc(prev_loaded, 16)
            sp.dma_start(prev_i[ROWS_LEFT:ROWS_LEFT + 1, BLOCKS - 1, 0:EDGES_LEFT],
                         dst[FULL + ROWS_LEFT * P - 1:EDGES - 1].rearrange("(p j) -> p j", p=1))\
              .then_inc(prev_loaded, 16)
            load_edges(sp, edge_weight, wgt_f, wgt_loaded)
            for k, w in enumerate((w1, w2, pool_w, final_w[:, 0:F], final_w[:, F:2 * F])):
                sp.dma_start(wraw[:, k, :], w).then_inc(par_loaded, 16)
            for k, b in enumerate((b1, b2, final_b, pool_b)):
                sp.dma_start(brow[0:1, k, :], b.rearrange("(a f) -> a f", a=1)).then_inc(par_loaded, 16)
            sp.wait_ge(x_clear, 1)
            sp.dma_start(xin[:, 0:TILES - 1, :],
                         x[0:(TILES - 1) * P, :].rearrange("(t p) f -> p t f", p=P)).then_inc(x_loaded, 16)
            sp.dma_start(xin[0:TAIL, TILES - 1, :], x[(TILES - 1) * P:NODES, :]).then_inc(x_loaded, 16)
            sp.wait_ge(masks_made, 3)
            sp.dma_start(*blocks_of(sum_mask, smask)).then_inc(masks_stored, 16)
            sp.dma_start(*blocks_of(max_mask, mmask)).then_inc(masks_stored, 16)
            sp.dma_start(*blocks_of(col_mask, cmask[:, :, :])).then_inc(masks_stored, 16)
            sp.wait_ge(z_made, TILES)
            sp.dma_start(table[0].rearrange("(t p) f -> p t f", p=P), own[:, :, :]).then_inc(z_stored, 16)
            sp.wait_ge(masks_stored, 48)

            for k in range(3):
                def short():
                    m = col_mask.rearrange("c j -> (c j)").rearrange("(a e) -> a e", a=1)

                    def turn(i, h, pair, first):
                        wait(sp, scanned[k], 2 * (i - 1))
                        sp.dma_start(col_m[:, h, :], m[0:1, bass.ds(i * TC, TC)].to_broadcast([P, TC]))\
                          .then_inc(mask_here[k][h], 16)
                        if not first:
                            store(i - 2, h)

                    def store(i, h):
                        sp.wait_ge(rows_ready[k], i + 1)
                        sp.dma_start(col_rows[k][bass.ds(i * TC, PC), :], rows[0:PC, h, 0, :])\
                          .then_inc(stored[k][h], 16)
                        sp.dma_start(col_rows[k][bass.ds(i * TC + PC, DC), :], rows[:, h, 1, :])\
                          .then_inc(stored[k][h], 16)

                    turn_pairs(sp, turn)
                    store(FT - 2, 0)
                    store(FT - 1, 1)

                def general():
                    m = (sum_mask, sum_mask, max_mask)[k].rearrange("c j -> (c j)").rearrange("(a e) -> a e", a=1)
                    out_rows = scan_rows[k].rearrange("(c p) f -> p c f", p=P)

                    def load_mask(g, s):
                        sp.dma_start(mask[:, s, :], m[0:1, bass.ds(g * GE, GE)].to_broadcast([P, GE]))\
                          .then_inc(mask_here[k][s], 16)

                    for s in range(SLOTS - 1):
                        load_mask(s, s)

                    def body(i, first, last):
                        for s in range(SLOTS):
                            g = i * SLOTS + s
                            if not (last and s > 0):
                                wait(sp, scanned[k], g)
                                load_mask(g + SLOTS - 1, (s + SLOTS - 1) % SLOTS)
                            sp.wait_ge(rows_ready[k], g + 1)
                            sp.dma_start(out_rows[:, bass.ds(g * GC, GC), :], rows[:, s, :, :])\
                              .then_inc(stored[k][s], 16)

                    turns(sp, ROUNDS, body)

                ways(sp, k, short, general)

                def node(i, first, last):
                    sp.wait_ge(tab_ready, i + k * TURNS + 1)
                    if k < 2:
                        sp.dma_start(table[k + 1].rearrange("(t p) f -> p t f", p=P)[:, bass.ds(i * TG, TG), :],
                                     tab[:, :, :]).then_inc(tab_stored, 16)
                    elif not last:
                        sp.dma_start(out[0:(TILES - 1) * P, :].rearrange("(t p) f -> p t f", p=P)
                                     [:, bass.ds(i * TG, TG), :], tab[:, :, :]).then_inc(tab_stored, 16)
                    else:
                        sp.dma_start(out[i * TG * P:(TILES - 1) * P, :].rearrange("(t p) f -> p t f", p=P),
                                     tab[:, 0:TG - 1, :]).then_inc(tab_stored, 16)
                        sp.dma_start(out[(TILES - 1) * P:NODES, :], tab[0:TAIL, TG - 1, :])\
                          .then_inc(tab_stored, 16)

                turns(sp, TURNS, node)
            sp.wait_ge(tab_stored, 16 * (3 * TURNS + 1))

        @block.gpsimd
        def _(pool):
            nc.gpsimd.iota(ids_i[:, :], pattern=[[P, TILES]], base=0, channel_multiplier=1).then_inc(ids_made, 1)
            nc.gpsimd.memset(dst_i[:, BLOCKS - 1, :], int(NOWHERE))
            nc.gpsimd.memset(prev_i[:, 0, :], -1)
            nc.gpsimd.memset(prev_i[:, BLOCKS - 1, :], -1)
            nc.gpsimd.memset(src_i[:, BLOCKS - 1, :], 0)
            nc.gpsimd.memset(wgt_f[:, BLOCKS - 1, :], 0.0).then_inc(edge_clear, 1)
            for t, base in ((ident, 0), (shift, 1), (wrap, 1 - P)):
                nc.gpsimd.memset(t[:, :], 0.0).then_inc(const_made, 1)
            pool.wait_ge(const_made, 3)
            for t, base in ((ident, 0), (shift, 1), (wrap, 1 - P)):
                nc.gpsimd.affine_select(out=t[:, :], in_=t[:, :], compare_op=ALU.not_equal, fill=1.0, base=base,
                                        pattern=[[-1, P]], channel_multiplier=1).then_inc(const_made, 1)
            nc.gpsimd.memset(ones_row[:, :], 1.0).then_inc(const_made, 1)
            nc.gpsimd.memset(eps[:, :], EPS).then_inc(const_made, 1)
            nc.gpsimd.memset(xin[:, TILES - 1, :], 0.0).then_inc(x_clear, 1)
            nc.gpsimd.iota(cell_no_i, pattern=[[P, CELL_BLOCKS], [0, P]], base=-MID, channel_multiplier=1)
            nc.gpsimd.iota(iota_i, pattern=[[1, WIN]], base=0, channel_multiplier=0)\
              .then_inc(iota_made, 1)

            pool.wait_ge(dst_stored, 16)
            for t in range(TILES):
                pool.wait_ge(rows_found, t + 1)
                if t >= 4:
                    pool.wait_ge(level_done, t - 3)
                nc.gpsimd.indirect_dma_start(level[:, t % 4, :], None, dst_rows[:, :],
                                             bass.IndirectOffsetOnAxis(ap=head_idx[:, t:t + 1], axis=0))\
                  .then_inc(level_got[t % 4], 16)

            for k in range(3):
                if k == 0:
                    pool.wait_ge(z_stored, 16)
                else:
                    pool.wait_ge(tab_stored, 16 * k * TURNS)

                def gather_nodes(from_rows):
                    def group(i, h, m):
                        pool.wait_ge(node_win_ready, k * WINDOWS + i + 1)
                        wait_alone(pool, agg_made, i + k * TURNS - 1)
                        for j in range(TG):
                            nc.gpsimd.indirect_dma_start(
                                node_got[:, h, j, :], None, from_rows[:, :],
                                bass.IndirectOffsetOnAxis(ap=node_win[:, h, j:j + 1], axis=0))\
                              .then_inc(node_gathered[h], 16)

                    node_steps(pool, group, lambda i, h, m: None)

                def fill(s, window):
                    for c in range(GC):
                        nc.gpsimd.indirect_dma_start(
                            got[:, s, c, :], None, table[k][:, :],
                            bass.IndirectOffsetOnAxis(ap=window[:, c:c + 1], axis=0))\
                          .then_inc(gathered[k][s], 16)

                def short():
                    def turn(i, h, pair, first):
                        pool.wait_ge(win_ready[k], i + 1)
                        for s in range(POOL_SL):
                            wait_alone(pool, turned[k], (i - 1) * POOL_SL + s + 1)
                            fill(s, idx_turn[:, h, s * GC:(s + 1) * GC])

                    turn_pairs(pool, turn)
                    for h in range(2):
                        pool.wait_ge(stored[k][h], 16 * FT)
                    gather_nodes(col_rows[k])

                def general():
                    def body(i, first, last):
                        for s in range(SLOTS):
                            g = i * SLOTS + s
                            pool.wait_ge(win_ready[k], g + 1)
                            wait_alone(pool, turned[k], g - SLOTS + 1)
                            fill(s, idx_win[:, s, :])

                    turns(pool, ROUNDS, body)
                    for s in range(SLOTS):
                        pool.wait_ge(stored[k][s], 16 * ROUNDS)
                    gather_nodes(scan_rows[k])

                ways(pool, k, short, general)

        @block.scalar
        def _(act):
            act.wait_ge(heads_spread, 1)
            act.wait_ge(idh_made, 1)
            for t in range(TILES):
                if t >= 2:
                    act.wait_ge(counted, t - 1)
                nc.scalar.activation(sign_junk[:, t % 2, :], bank_d[:, 0, 0:HEADS], ACT.Sign, scale=-1.0,
                                     bias=idh[:, t:t + 1], accum_out=signs[:, t:t + 1]).then_inc(counted, 1)
            act.wait_ge(deg_done, 1)
            nc.scalar.activation(sdeg[:, :], deg[:, :], ACT.Sqrt).then_inc(root_done, 1)
            act.wait_ge(dinv_done, 1)
            act.wait_ge(x_loaded, 32)
            for t in range(0, TILES, 2):
                nc.scalar.activation(own[:, t, :], xin[:, t, :], ACT.Copy, scale=dinv[:, t:t + 1])\
                  .then_inc(z_made, 1)

            for k in range(3):
                def short():
                    act.wait_ge(z_made, TILES)
                    if k == 0:
                        act.wait_ge(masks_stored, 48)
                        act.wait_ge(prep, PREP)
                        act.wait_ge(flip_copied, FLIPPED)
                    for n in range(TURNS):
                        g = slice(n * TG, (n + 1) * TG)
                        nc.scalar.copy(parts[:, 0, g, :], own[:, g, :]).then_inc(part_hi[k], 1)
                        act.wait_ge(rest_hi[k], n + 1)
                        nc.scalar.copy(parts[:, 1, g, :], rest[:, :, :]).then_inc(part_mid[k], 1)

                    def keep_rows(i, h, pair):
                        act.wait_ge(turned_back[k], i + 1)
                        wait(act, stored[k][h], 32 * pair)
                        nc.scalar.copy(rows[0:PC, h, 0, :], bank_b[0:PC, 0, 0:P])
                        nc.scalar.copy(rows[:, h, 1, :], bank_b[:, 0, P:2 * P])\
                           .then_inc(rows_ready[k], 1)

                    def turn(i, h, pair, first):
                        for j in range(DENSE_CH):
                            act.wait_ge(built[k], i * DENSE_CH + j + 1)
                            if j == 0:
                                wait(act, applied[k], i - 1)
                            nc.scalar.copy(counts[:, h, :, j * WIN:(j + 1) * WIN],
                                           build[j % 2].rearrange("p (a l) -> p a l", l=WIN)).then_inc(kept[k], 1)
                            if j == 12 and not first:
                                keep_rows(i - 2, h, pair - 1)

                    turn_pairs(act, turn)
                    keep_rows(FT - 2, 0, FT // 2 - 1)
                    keep_rows(FT - 1, 1, FT // 2 - 1)

                def general():
                    def keep_rows(b, g, uses):
                        act.wait_ge(turned_back[k], g + 1)
                        wait(act, stored[k][b], uses * 16)
                        nc.scalar.copy(rows[:, b, :, :], bank_b[:, b % 2, :].rearrange("p (c f) -> p c f", c=GC))\
                           .then_inc(rows_ready[k], 1)

                    def body(i, first, last):
                        for s in range(SLOTS):
                            g = i * SLOTS + s
                            if k == 2:
                                act.wait_ge(gathered[k][s], (i + 1) * 16 * GC)
                                for c in range(GC):
                                    a = nc.scalar.activation(got[:, s, c, :], got[:, s, c, :], ACT.Copy,
                                                             scale=wgt_t[:, bass.ds(g * GC + c, 1)])
                                a.then_inc(scaled, 1)
                            if s > 0 or not first:
                                keep_rows((s - 1) % SLOTS, g - 1, i - (1 if s == 0 else 0))

                    turns(act, ROUNDS, body)
                    keep_rows(SLOTS - 1, GROUPS - 1, ROUNDS - 1)

                ways(act, k, short, general)

                def front(i, h, m):
                    n = i + k * TURNS
                    act.wait_ge(agg_turned, n + 1)
                    nc.scalar.copy(agg_t[:, :, :], na).then_inc(agg_t_copied, 1)

                def back(i, h, m):
                    n = i + k * TURNS
                    group = slice(None), bass.ds(i * TG, TG), slice(None)
                    if k == 0:
                        act.wait_ge(tab_ready, n + 1)
                        nc.scalar.copy(own[group], tab[:, :, :]).then_inc(own_done, 1)
                        return
                    act.wait_ge(mv_made, (n - TURNS + 1) * TG)
                    nc.scalar.activation(sd[:, :], mv[:, :, 1], ACT.Sqrt, bias=eps[:, 0:1]).then_inc(sd_made, 1)
                    if k == 1:
                        act.wait_ge(normed, i + 1)
                        nc.scalar.copy(xin[group], xn[:, :, :]).then_inc(x1_kept, 1)
                        act.wait_ge(x1_turned, i + 1)
                        nc.scalar.copy(agg_t[:, :, :], nd).then_inc(x1_t_copied, 1)
                        act.wait_ge(heads_out, i + 1)
                        wait(act, tab_stored, 16 * n)
                        nc.scalar.copy(tab[:, :, :], ncc).then_inc(tab_ready, 1)
                        nc.scalar.copy(own[group], nd).then_inc(half_kept, 1)

                node_steps(act, front, back)

        @block.tensor
        def _(pe):
            pe.wait_ge(const_made, 8)
            pe.wait_ge(heads_cast, 1)
            nc.tensor.matmul(bank_d[:, 0, 0:HEADS], ones_row[:, :], heads_f[:, :], start=True, stop=True)\
              .then_inc(heads_spread, 1)
            for n, (kind, t, b, _) in enumerate(flips):
                if b == 0:
                    pe.wait_ge(*flip_needs[kind])
                if n >= 2:
                    pe.wait_ge(flip_copied, n - 1)
                nc.tensor.transpose(bank_a[:, n % 2, 0:P], t[:, b, :], ident[:, :]).then_inc(flipped, 1)
            pe.wait_ge(par_loaded, 9 * 16)
            nc.tensor.matmul(bank_c[:, 0, :], ones_row[:, :], brow[0:1, :, :].rearrange("a k f -> a (k f)"),
                             start=True, stop=True).then_inc(bias_spread, 1)
            pe.wait_ge(prep, SPAN_STEP)
            nc.tensor.transpose(bank_c[0:1, 1, 0:P], spanm[:, 0:1], ident[:, :]).then_inc(span_turned, 1)
            pe.wait_ge(short_known, 1)
            nc.tensor.matmul(bank_c[:, 1, P:P + 1], ones_row[:, :], short_f[:, :], start=True, stop=True)\
              .then_inc(short_spread, 1)
            pe.wait_ge(count_done, TILES + 1)
            nc.tensor.matmul(bank_b[:, 0, 0:TILES], shift[:, :], count[:, 1:TILES + 1], start=True, stop=False)
            nc.tensor.matmul(bank_b[:, 0, 0:TILES], wrap[:, :], count[:, 0:TILES], start=False, stop=True)\
              .then_inc(shifted, 1)
            pe.wait_ge(deg_done, 1)
            pe.wait_ge(bias_kept, 1)
            pe.wait_ge(idx_step, 1)
            pe.wait_ge(flip_copied, len(flips))

            for k in range(3):
                def short():
                    def apply(i, h, n, pieces):
                        if n == 0:
                            pe.wait_ge(kept[k], (i + 1) * DENSE_CH)
                            wait(pe, scanned[k], 2 * (i - 1))
                            pe.wait_ge(parts_done[k], TURNS)
                        lo, hi = TILES * n // pieces, TILES * (n + 1) // pieces
                        for a in range(lo, hi):
                            for q in range(3):
                                mm = nc.tensor.matmul(bank_a[:, h, 0:DC], parts[:, q, a, :],
                                                      counts[:, h, a, :], start=(a == 0 and q == 0),
                                                      stop=(a == TILES - 1 and q == 2))
                        if n == pieces - 1:
                            mm.then_inc(applied[k], 1)

                    def products(i, h, s):
                        wait(pe, scanned[k], 2 * i - 1)
                        pe.wait_ge(gathered[k][s], (i + 1) * 16 * GC)
                        pe.wait_ge(off_ready[k], i + 1)
                        for c in range(s * GC, (s + 1) * GC):
                            mm = nc.tensor.matmul(bank_d[:, 1, c * WIN:(c + 1) * WIN], got[:, s, c % GC, :],
                                                  hot_off[:, h, c, :], start=True, stop=True)
                        mm.then_inc(turned[k], 1)

                    def rows_back(i, h):
                        pe.wait_ge(scanned[k], 2 * i + 2)
                        wait(pe, rows_ready[k], i)
                        nc.tensor.transpose(bank_b[0:PC, 0, 0:P], scan[:, h, 0:PC], ident[:, :])
                        nc.tensor.transpose(bank_b[:, 0, P:2 * P], scan[:, h, PC:TC],
                                            ident[:, :]).then_inc(turned_back[k], 1)

                    def turn(i, h, pair, first):
                        for j in range(DENSE_CH):
                            pe.wait_ge(hot_ready[k], i * DENSE_CH + j + 1)
                            wait(pe, kept[k], i * DENSE_CH + j - 1)
                            nc.tensor.matmul(build[j % 2], hot_low[:, j % 4, :], hot_cell[:, j % 4, :],
                                             start=True, stop=True).then_inc(built[k], 1)
                            if not (first and h == 0):
                                apply(i - 1, 1 - h, j, DENSE_CH)
                                if j in PRODUCTS_AT:
                                    products(i - 1, 1 - h, PRODUCTS_AT.index(j))
                            if j == 9 and not first:
                                rows_back(i - 2, h)

                    for b in range(CELL_BLOCKS):
                        n = min(P, TILES * WIN - b * P)
                        mm = nc.tensor.transpose(iota[:, b * P:b * P + n], cell_no[0:n, b, :], ident_b[0:n, 0:n])
                    mm.then_inc(iota_spread, 1)
                    turn_pairs(pe, turn)
                    for n in range(DENSE_CH):
                        apply(FT - 1, 1, n, DENSE_CH)
                        if n in PRODUCTS_AT:
                            products(FT - 1, 1, PRODUCTS_AT.index(n))
                    rows_back(FT - 2, 0)
                    rows_back(FT - 1, 1)
                    pe.wait_ge(rows_ready[k], FT)

                def general():
                    def back(n, q):
                        pe.wait_ge(scanned[k], n + 1)
                        wait(pe, rows_ready[k], n - 1)
                        for c in range(GC):
                            a = nc.tensor.transpose(bank_b[:, q, c * P:(c + 1) * P], scan[:, q, c * P:(c + 1) * P],
                                                    ident[:, :])
                        a.then_inc(turned_back[k], 1)

                    def body(i, first, last):
                        for s in range(SLOTS):
                            g = i * SLOTS + s
                            if k == 2:
                                pe.wait_ge(scaled, g + 1)
                            else:
                                pe.wait_ge(gathered[k][s], (i + 1) * 16 * GC)
                            wait(pe, scanned[k], g - 1)
                            for c in range(GC):
                                a = nc.tensor.transpose(bank_a[:, s % 2, c * P:(c + 1) * P], got[:, s, c, :],
                                                        ident[:, :])
                            a.then_inc(turned[k], 1)
                            if s > 0 or not first:
                                back(g - 1, (s - 1) % 2)

                    turns(pe, ROUNDS, body)
                    back(GROUPS - 1, (SLOTS - 1) % 2)
                    pe.wait_ge(rows_ready[k], GROUPS)

                ways(pe, k, short, general)

                def front(i, h, m):
                    n = i + k * TURNS
                    pe.wait_ge(agg_made, n + 1)
                    wait(pe, agg_t_copied, n)
                    for j in range(TG):
                        a = nc.tensor.transpose(na[:, j, :], agg[:, j, :], ident[:, :])
                    a.then_inc(agg_turned, 1)
                    pe.wait_ge(agg_t_copied, n + 1)
                    wait(pe, res_made, n)
                    for j in range(TG):
                        a = nc.tensor.matmul(nb[:, j, :], agg_t[:, j, :], wt[:, (0, 1, 4)[k], :],
                                             start=True, stop=True)
                    a.then_inc(linear_done, 1)

                def back(i, h, m):
                    if k != 1:
                        return
                    pe.wait_ge(normed, i + 1)
                    wait(pe, half_kept, i)
                    for j in range(TG):
                        a = nc.tensor.transpose(nd[:, j, :], xn[:, j, :], ident[:, :])
                    a.then_inc(x1_turned, 1)
                    pe.wait_ge(x1_t_copied, i + 1)
                    pe.wait_ge(tab_ready, i + TURNS)
                    for j in range(TG):
                        nc.tensor.matmul(nd[:, j, :], agg_t[:, j, :], wt[:, 3, :], start=True, stop=True)
                        a = nc.tensor.matmul(ncc[:, j, :], agg_t[:, j, :], wt[:, 2, :], start=True, stop=True)
                    a.then_inc(heads_out, 1)

                node_steps(pe, front, back)

        @block.vector
        def _(dve):
            steps = [0]

            def step(ins):
                ins.then_inc(prep, 1)
                steps[0] += 1
                dve.wait_ge(prep, steps[0])

            dve.wait_ge(heads_loaded, 16)
            nc.vector.tensor_copy(heads_f[:, :], heads_i[:, :]).then_inc(heads_cast, 1)
            dve.wait_ge(ids_made, 1)
            nc.vector.tensor_copy(ids[:, :], ids_i[:, :]).then_inc(ids_made, 1)
            dve.wait_ge(ids_made, 2)
            nc.vector.tensor_scalar(idh[:, :], ids[:, :], 0.5, None, ALU.add).then_inc(idh_made, 1)
            nc.vector.memset(count[:, 0:1], 0.0).then_inc(count_done, 1)
            dve.wait_ge(dst_loaded, 48)
            nc.vector.tensor_copy(dst_f[:, :, :], dst_i[:, :, :]).then_inc(dst_cast, 1)
            dve.wait_ge(src_loaded, 48)
            nc.vector.tensor_copy(src_f[:, :, :], src_i[:, :, :]).then_inc(src_cast, 1)

            def prepare_offsets():
                dve.wait_ge(dst_cast, 1)
                step(nc.vector.tensor_tensor(off_f[:, :, :], dst_f[:, :, :],
                                             dst_f[:, :, 0:1].to_broadcast([P, BLOCKS, P]), ALU.subtract))

            def prepare_masks():
                dve.wait_ge(prev_loaded, 80)
                nc.vector.tensor_tensor(smask[:, :, :], dst_i[:, :, :], prev_i[:, :, :], ALU.is_equal)\
                  .then_inc(masks_made, 1)

            def prepare_max_mask():
                dve.wait_ge(masks_made, 1)
                nc.vector.tensor_scalar(mmask[:, :, :], smask[:, :, :], 1.0, -RESET, ALU.subtract, ALU.mult)\
                  .then_inc(masks_made, 1)

            def prepare_span():
                step(nc.vector.scalar_tensor_tensor(out=cell_f[:, :, :], in0=dst_f[:, :, :], scalar=NOWHERE,
                                                    in1=off_f[:, :, :], op0=ALU.is_lt, op1=ALU.mult))
                step(nc.vector.tensor_reduce(span[:, :], cell_f[:, :, :], AX.X, ALU.max))
                step(nc.vector.tensor_reduce(spanm[:, :], span[:, :], AX.X, ALU.max))

            def prepare_low():
                dve.wait_ge(masks_made, 1)
                step(nc.vector.tensor_scalar(prev_i[:, :, :], src_i[:, :, :], P - 1, None, ALU.bitwise_and))
                dve.wait_ge(flip_copied, BLOCKS)
                step(nc.vector.tensor_copy(src_f[:, :, :], prev_i[:, :, :]))

            def prepare_cell():
                step(nc.vector.tensor_tensor(src_i[:, :, :], src_i[:, :, :], prev_i[:, :, :], ALU.subtract))
                step(nc.vector.scalar_tensor_tensor(out=cell_f[:, :, :], in0=src_i[:, :, :], scalar=WIN / P,
                                                    in1=off_f[:, :, :], op0=ALU.mult, op1=ALU.add))
                step(nc.vector.tensor_scalar(cell_f[:, :, :], cell_f[:, :, :], -float(MID), None, ALU.add))

            def prepare_way():
                dve.wait_ge(span_turned, 1)
                step(nc.vector.tensor_reduce(spanr[:, :], bank_c[0:1, 1, 0:P], AX.X, ALU.max))
                step(nc.vector.tensor_scalar(short_f[:, :], spanr[:, :], WIN - 0.5, None, ALU.is_lt))
                nc.vector.tensor_copy(short_i[:, :], short_f[:, :]).then_inc(short_known, 1)

            def prepare_columns():
                dve.wait_ge(iota_made, 1)
                dve.wait_ge(const_made, 8)
                nc.vector.tensor_copy(cell_no[:, :, :], cell_no_i.rearrange("p (b c) -> p b c", c=P))
                nc.vector.tensor_copy(ident_b[:, :], ident[:, :])
                step(nc.vector.tensor_copy(iota_f[:, :], iota_i))
                step(nc.vector.tensor_tensor(cmask[:, :, :],
                                             iota_f[:, :].rearrange("p (a l) -> p a l", a=1)
                                             .to_broadcast([P, BLOCKS, WIN]),
                                             span[:, :].rearrange("p (b l) -> p b l", l=1)
                                             .to_broadcast([P, BLOCKS, WIN]), ALU.is_gt))
                nc.vector.tensor_copy(cmask[:, :, 0:1], smask[:, :, 0:1]).then_inc(masks_made, 1)

            def take(n):
                kind, _, b, to = flips[n]
                dve.wait_ge(flipped, n + 1)
                nc.vector.tensor_copy(to, bank_a[:, n % 2, 0:P]).then_inc(flip_copied, 1)

            def find_row(t):
                dve.wait_ge(counted, t + 1)
                nc.vector.tensor_scalar(head_row[:, t:t + 1], signs[:, t:t + 1], 0.5, HEADS / 2 - 1.0,
                                        ALU.mult, ALU.add).then_inc(deg_step, 1)
                dve.wait_ge(deg_step, 2 * t + 1)
                nc.vector.tensor_scalar(head_row[:, t:t + 1], head_row[:, t:t + 1], 0.0, None, ALU.max)\
                   .then_inc(deg_step, 1)
                dve.wait_ge(deg_step, 2 * t + 2)
                nc.vector.tensor_copy(head_idx[:, t:t + 1], head_row[:, t:t + 1]).then_inc(rows_found, 1)

            def count_row(t):
                dve.wait_ge(level_got[t % 4], 16 * (t // 4 + 1))
                nc.vector.tensor_copy(h4[:, t, :], level[:, t % 4, 0:GE:P])
                nc.vector.tensor_scalar(level_junk[:, :], level[:, t % 4, :], ids[:, t:t + 1], None, ALU.is_le,
                                        ALU.add, accum_out=inner[:, t:t + 1]).then_inc(level_done, 1)
                dve.wait_ge(level_done, t + 1)
                nc.vector.scalar_tensor_tensor(out=count[:, t + 1:t + 2], in0=head_row[:, t:t + 1], scalar=float(GE),
                                               in1=inner[:, t:t + 1], op0=ALU.mult, op1=ALU.add)\
                   .then_inc(count_done, 1)

            between = [prepare_offsets, prepare_masks, prepare_max_mask, prepare_span]
            between += [lambda n=n: take(n) for n in range(BLOCKS)]
            between += [prepare_low, prepare_cell, prepare_columns]
            between += [lambda n=n: take(n) for n in range(BLOCKS, len(flips))]
            LAG = 4
            spread = 0
            for t in range(TILES + LAG):
                if t < TILES:
                    find_row(t)
                if t >= LAG:
                    count_row(t - LAG)
                upto = len(between) * (t + 1) // (TILES + LAG)
                for piece in between[spread:upto]:
                    piece()
                spread = upto
            dve.wait_ge(bias_spread, 1)
            nc.vector.tensor_copy(bias[:, :, :], bank_c[:, 0, :].rearrange("p (k f) -> p k f", k=4))\
              .then_inc(bias_kept, 1)
            prepare_way()
            assert steps[0] == PREP, steps

            dve.wait_ge(shifted, 1)
            dve.wait_ge(count_done, TILES + 1)
            nc.vector.tensor_tensor(indeg[:, :], count[:, 1:TILES + 1], bank_b[:, 0, 0:TILES], ALU.subtract)\
              .then_inc(deg_step, 1)
            n = 2 * TILES + 1
            dve.wait_ge(deg_step, n)
            nc.vector.tensor_scalar(deg[:, :], indeg[:, :], 1.0, None, ALU.add).then_inc(deg_done, 1)
            nc.vector.tensor_scalar(has[:, :], indeg[:, :], 1.0, None, ALU.min)
            nc.vector.tensor_scalar(last_f[:, :], count[:, 1:TILES + 1], -1.0, 0.0, ALU.add, ALU.max)\
              .then_inc(deg_step, 1)
            dve.wait_ge(root_done, 1)
            nc.vector.reciprocal(dinv[:, :], sdeg[:, :]).then_inc(dinv_done, 1)
            dve.wait_ge(dinv_done, 1)
            dve.wait_ge(x_loaded, 32)
            for t in range(1, TILES, 2):
                nc.vector.tensor_scalar(own[:, t, :], xin[:, t, :], dinv[:, t:t + 1], None, ALU.mult)\
                   .then_inc(z_made, 1)

            def first_windows(k):
                for s in range(SLOTS):
                    nc.vector.tensor_copy(idx_win[:, s, :], src_t[:, s * GC:(s + 1) * GC])\
                       .then_inc(win_ready[k], 1)

            dve.wait_ge(flip_copied, len(flips))

            m = [0]

            def then(ins):
                ins.then_inc(idx_step, 1)
                m[0] += 1
                dve.wait_ge(idx_step, m[0])

            dve.wait_ge(short_spread, 1)
            then(nc.vector.tensor_copy(short_p[:, :], bank_c[:, 1, P:P + 1]))
            then(nc.vector.tensor_tensor(le4[:, :, :], h4[:, :, :],
                                         ids[:, :].rearrange("p (t c) -> p t c", c=1).to_broadcast([P, TILES, GC]),
                                         ALU.is_le))
            then(nc.vector.tensor_reduce(nle[:, :], le4[:, :, :], AX.X, ALU.add))
            then(nc.vector.tensor_tensor(h4[:, :, :], h4[:, :, :], le4[:, :, :], ALU.mult))
            then(nc.vector.tensor_reduce(first_dst[:, :], h4[:, :, :], AX.X, ALU.max))
            then(nc.vector.scalar_tensor_tensor(out=pos[:, :], in0=head_row[:, :], scalar=float(GC), in1=nle[:, :],
                                                op0=ALU.mult, op1=ALU.add))
            then(nc.vector.tensor_scalar(pos[:, :], pos[:, :], -1.0, 0.0, ALU.add, ALU.max))
            then(nc.vector.tensor_tensor(posd[:, :], ids[:, :], first_dst[:, :], ALU.subtract))
            then(nc.vector.tensor_scalar(posd[:, :], posd[:, :], WIN - 1.0, None, ALU.min))
            then(nc.vector.scalar_tensor_tensor(out=pos[:, :], in0=pos[:, :], scalar=float(WIN), in1=posd[:, :],
                                                op0=ALU.mult, op1=ALU.add))
            then(nc.vector.tensor_tensor(posd[:, :], pos[:, :], last_f[:, :], ALU.subtract))
            then(nc.vector.scalar_tensor_tensor(out=posd[:, :], in0=posd[:, :], scalar=short_p[:, 0:1],
                                                in1=last_f[:, :], op0=ALU.mult, op1=ALU.add))
            for w, t in ((0, posd), (1, last_f)):
                nc.vector.tensor_copy(last_idx[:, w, 0:TILES], t[:, :])
                then(nc.vector.tensor_copy(last_idx[:, w, TILES:TILES + 2 * TG], t[:, 0:2 * TG]))
            dve.wait_ge(bias_kept, 1)
            dve.wait_ge(z_made, TILES)
            for t in range(TILES):
                nc.vector.tensor_tensor(xin[:, t, :], xin[:, t, :], bias[:, 1, :], ALU.add).then_inc(x_biased, 1)

            for k in range(3):
                op0, op1 = (ALU.mult, ALU.add) if k < 2 else (ALU.add, ALU.max)

                wait(dve, node_win_ready, k * WINDOWS)
                for h in range(2):
                    nc.vector.tensor_copy(node_win[:, h, :], last_idx[:, k // 2, h * TG:(h + 1) * TG])\
                       .then_inc(node_win_ready, 1)
                if k == 2:
                    dve.wait_ge(half_kept, TURNS)
                    for n in range(TURNS):
                        g = slice(n * TG, (n + 1) * TG)
                        nc.vector.tensor_tensor(own[:, g, :], own[:, g, :], bias[:, 2:3, :].to_broadcast([P, TG, F]),
                                                ALU.add).then_inc(half_biased, 1)
                def short():
                    if k == 0:
                        dve.wait_ge(masks_stored, 48)
                    def next_window(i, h):
                        for s in range(POOL_SL):
                            wait_alone(dve, gathered[k][s], (i - 1) * 16 * GC)
                        nc.vector.tensor_copy(idx_turn[:, h, :], src_t[:, bass.ds(i * TURN_CH, POOL_CH)])\
                           .then_inc(win_ready[k], 1)

                    next_window(0, 0)
                    for n in range(TURNS):
                        g = slice(n * TG, (n + 1) * TG)
                        dve.wait_ge(part_hi[k], n + 1)
                        wait(dve, parts_done[k], n)
                        nc.vector.tensor_tensor(rest[:, :, :], own[:, g, :], parts[:, 0, g, :], ALU.subtract)\
                           .then_inc(rest_hi[k], 1)
                        dve.wait_ge(part_mid[k], n + 1)
                        dve.wait_ge(rest_hi[k], n + 1)
                        nc.vector.tensor_tensor(parts[:, 2, g, :], rest[:, :, :], parts[:, 1, g, :], ALU.subtract)\
                           .then_inc(parts_done[k], 1)

                    dve.wait_ge(iota_spread, k + 1)

                    def scan_turn(i, h, pair, first):
                        dve.wait_ge(applied[k], i + 1)
                        dve.wait_ge(turned[k], POOL_SL * (i + 1))
                        dve.wait_ge(mask_here[k][h], 16 * (pair + 1))
                        wait(dve, turned_back[k], i - 1)
                        wait(dve, scanned[k], 2 * i)
                        init = 0.0 if first and h == 0 else scan[:, 1 - h, TC - 1:TC]
                        nc.vector.tensor_tensor_scan(scan[:, h, 0:PC], col_m[:, h, 0:PC], bank_d[:, 1, 0:PC], init,
                                                     op0, op1).then_inc(scanned[k], 1)
                        dve.wait_ge(scanned[k], 2 * i + 1)
                        nc.vector.tensor_tensor_scan(scan[:, h, PC:TC], col_m[:, h, PC:TC], bank_a[:, h, 0:DC],
                                                     scan[:, h, PC - 1:PC], op0, op1).then_inc(scanned[k], 1)

                    def turn(i, h, pair, first):
                        base = i * TURN_CH
                        wait(dve, turned[k], POOL_SL * (i - 1))
                        nc.vector.tensor_tensor(
                            hot_off[:, h, :, :],
                            off_t[:, bass.ds(base, POOL_CH)].rearrange("p (c l) -> p c l", l=1)
                            .to_broadcast([P, POOL_CH, WIN]),
                            iota_f[:, :].rearrange("p (a l) -> p a l", a=1).to_broadcast([P, POOL_CH, WIN]),
                            ALU.is_equal).then_inc(off_ready[k], 1)
                        for j in range(DENSE_CH):
                            c = base + (POOL_CH + j)
                            wait(dve, built[k], i * DENSE_CH + j - 3)
                            nc.vector.tensor_scalar(hot_low[:, j % 4, :], iota[:, MID:MID + P], low_t[:, bass.ds(c, 1)],
                                                    None, ALU.is_equal)
                            nc.vector.tensor_scalar(hot_cell[:, j % 4, :], iota, cell_t[:, bass.ds(c, 1)],
                                                    None, ALU.is_equal).then_inc(hot_ready[k], 1)
                            if j == 2 and not first:
                                scan_turn(i - 2, h, pair - 1, False if not isinstance(pair, int) else pair == 1)
                            if j == 6 and not (isinstance(i, int) and i == FT - 1):
                                next_window(i + 1, 1 - h)

                    turn_pairs(dve, turn)
                    scan_turn(FT - 2, 0, FT // 2 - 1, False)
                    scan_turn(FT - 1, 1, FT // 2 - 1, False)

                def general():
                    first_windows(k)

                    def body(i, first, last):
                        for s in range(SLOTS):
                            g = i * SLOTS + s
                            if not last:
                                wait_alone(dve, gathered[k][s], (i + 1) * 16 * GC)
                                nc.vector.tensor_copy(idx_win[:, s, :], src_t[:, bass.ds((g + SLOTS) * GC, GC)])\
                                   .then_inc(win_ready[k], 1)
                            dve.wait_ge(turned[k], g + 1)
                            dve.wait_ge(mask_here[k][s], (i + 1) * 16)
                            wait(dve, turned_back[k], g - 1)
                            wait(dve, scanned[k], g)
                            init = 0.0 if first and s == 0 else scan[:, (s - 1) % 2, GE - 1:GE]
                            nc.vector.tensor_tensor_scan(scan[:, s % 2, :], mask[:, s, :], bank_a[:, s % 2, :],
                                                         init, op0, op1).then_inc(scanned[k], 1)

                    turns(dve, ROUNDS, body)

                ways(dve, k, short, general)

                if k == 0:
                    dve.wait_ge(x_biased, TILES)
                elif k == 1:
                    dve.wait_ge(own_done, TURNS)
                else:
                    dve.wait_ge(x1_kept, TURNS)
                    dve.wait_ge(half_biased, TURNS)

                def front(i, h, m):
                    n = i + k * TURNS
                    dve.wait_ge(node_gathered[h], (k * (TURNS // 2 + 1 - h) + m + 1) * 16 * TG)
                    wait(dve, agg_turned, n)
                    for j in range(TG):
                        t = i * TG + j
                        row = node_got[:, h, j, :]
                        if k < 2:
                            a = nc.vector.scalar_tensor_tensor(out=agg[:, j, :], in0=row,
                                                               scalar=has[:, bass.ds(t, 1)],
                                                               in1=one(own, t), op0=ALU.mult, op1=ALU.add)
                        else:
                            a = nc.vector.tensor_tensor(agg[:, j, :], row, bias[:, 3, :], ALU.add)
                    if k == 2:
                        a.then_inc(agg_pre, 1)
                        dve.wait_ge(agg_pre, i + 1)
                        for j in range(TG):
                            a = nc.vector.tensor_scalar(agg[:, j, :], agg[:, j, :], 0.0,
                                                        has[:, bass.ds(i * TG + j, 1)], ALU.max, ALU.mult)
                    a.then_inc(agg_made, 1)
                    nc.vector.tensor_copy(node_win[:, h, :], last_idx[:, k // 2, bass.ds((i + 2) * TG, TG)])\
                       .then_inc(node_win_ready, 1)

                def back(i, h, m):
                    n = i + k * TURNS
                    dve.wait_ge(linear_done, n + 1)
                    if k == 0:
                        wait(dve, tab_stored, n * 16)
                        wait(dve, own_done, i)
                        for j in range(TG):
                            t = i * TG + j
                            a = nc.vector.scalar_tensor_tensor(out=res[:, j, :], in0=nb[:, j, :],
                                                               scalar=dinv[:, bass.ds(t, 1)], in1=bias[:, 0, :],
                                                               op0=ALU.mult, op1=ALU.add)
                        a.then_inc(res_made, 1)
                        dve.wait_ge(res_made, n + 1)
                        for j in range(TG):
                            t = i * TG + j
                            a = nc.vector.tensor_scalar(tab[:, j, :], res[:, j, :], 0.0, dinv[:, bass.ds(t, 1)],
                                                        ALU.max, ALU.mult)
                        a.then_inc(tab_ready, 1)
                        return
                    old = xin[:, bass.ds(i * TG, TG), :]
                    if k == 1:
                        wait(dve, normed, i)
                    else:
                        wait(dve, tab_ready, n)
                    if k == 1:
                        for j in range(TG):
                            t = i * TG + j
                            a = nc.vector.scalar_tensor_tensor(out=res[:, j, :], in0=nb[:, j, :],
                                                               scalar=dinv[:, bass.ds(t, 1)], in1=one(xin, t),
                                                               op0=ALU.mult, op1=ALU.add)
                        a.then_inc(res_made, 1)
                    else:
                        nc.vector.tensor_tensor(res[:, :, :], nb, own[:, bass.ds(i * TG, TG), :], ALU.add)\
                           .then_inc(res_pre, 1)
                        dve.wait_ge(res_pre, i + 1)
                        nc.vector.scalar_tensor_tensor(out=res[:, :, :], in0=res[:, :, :], scalar=0.0, in1=old,
                                                       op0=ALU.max, op1=ALU.add).then_inc(res_made, 1)
                    dve.wait_ge(res_made, n + 1)
                    m = i + (k - 1) * TURNS
                    for j in range(TG):
                        nc.vector.bn_stats(stats[:, j, :], res[:, j, :]).then_inc(stats_made, 1)
                    wait_alone(dve, stats_made, m * TG + TG)
                    for j in range(TG):
                        nc.vector.bn_aggr(mv[:, j, :], stats[:, j, :]).then_inc(mv_made, 1)
                    dve.wait_ge(sd_made, m + 1)
                    nc.vector.reciprocal(rstd[:, :], sd[:, :]).then_inc(rstd_made, 1)
                    dve.wait_ge(rstd_made, m + 1)
                    if k == 2:
                        wait(dve, tab_stored, n * 16)
                    else:
                        wait(dve, x1_kept, i)
                        wait(dve, x1_turned, i)
                    for j in range(TG):
                        to = xn[:, j, :] if k == 1 else tab[:, j, :]
                        a = nc.vector.tensor_scalar(to, res[:, j, :], mv[:, j, 0:1], rstd[:, j:j + 1],
                                                    ALU.subtract, ALU.mult)
                    a.then_inc(normed if k == 1 else tab_ready, 1)

                node_steps(dve, front, back)


_INS = ["x", "src", "dst", "edge_weight", "L0_gnn_W1", "L0_gnn_b1", "L0_gnn_W2", "L0_gnn_b2",
        "L1_gnn_pool_w", "L1_gnn_pool_b", "L1_gnn_final_w", "L1_gnn_final_b"]


def kernel(**inputs):
    import numpy as _np
    import concourse.bacc as _bacc
    from concourse import mybir as _mybir
    from concourse.bass_utils import run_bass_kernel_spmd as _run

    nc = _bacc.Bacc("TRN2", target_bir_lowering=False, num_devices=1)
    arrays, args = {}, []
    for name in _INS:
        a = _np.ascontiguousarray(inputs[name])
        arrays[f"in_{name}"] = a
        args.append(nc.dram_tensor(f"in_{name}", a.shape, _mybir.dt.from_np(a.dtype), kind="ExternalInput").ap())
    result = nc.dram_tensor("out_0", (NODES, F), F32, kind="ExternalOutput").ap()
    program(nc, *args, result)
    r = _run(nc, [arrays], core_ids=[0])
    return r.results[0]["out_0"]
```

```python
from contextlib import ExitStack

import concourse.bass as bass
from concourse import mybir

P = 128
F = 128
NODES = 6250
EDGES = 206250
TILES = -(-NODES // P)
NPAD = TILES * P
TAIL = NODES - (TILES - 1) * P
GC = 4
GE = GC * P
SLOTS = 4
ROUNDS = -(-EDGES // (GE * SLOTS))
Z_PART = TILES // 2
GROUPS = ROUNDS * SLOTS
WIN = 7
POOL_CH = 24
DENSE_CH = 32
TURN_CH = POOL_CH + DENSE_CH
CELLS = TILES * WIN
CELL_BLOCKS = -(-CELLS // P)
MID = CELLS // 4 * 2
UNITS = POOL_CH // GC
FT = -(-EDGES // (P * TURN_CH))
PC, DC = POOL_CH * WIN, DENSE_CH * WIN
TC = PC + DC
BACK = [min(P, TC - b * P) for b in range(-(-TC // P))]
BLOCKS = -(-max(GROUPS * GC, FT * TURN_CH) // P)
CHUNKS = BLOCKS * P
FULL = (BLOCKS - 1) * P * P
ROWS_LEFT = (EDGES - FULL) // P
EDGES_LEFT = EDGES - FULL - ROWS_LEFT * P
HEADS = -(-EDGES // GE)
TG = 7
TURNS = TILES // TG
PRODUCTS_AT = (5, 10, 14, 19, 23, 28)
RESET = -3.3e38
NOWHERE = 1.0e5
EPS = 1e-5

ALU = mybir.AluOpType
ACT = mybir.ActivationFunctionType
AX = mybir.AxisListType
F32 = mybir.dt.float32
BF16 = mybir.dt.bfloat16
I32 = mybir.dt.int32
I16 = mybir.dt.int16
U32 = mybir.dt.uint32


def program(nc, x, src, dst, edge_weight, w1, b1, w2, b2, pool_w, pool_b, final_w, final_b, out):
    with ExitStack() as ctx:
        def sb(name, shape, dt=F32):
            return ctx.enter_context(nc.sbuf_tensor(name, shape, dt))

        def ps(name, shape, dt=F32):
            return ctx.enter_context(nc.psum_tensor(name, shape, dt))

        def sem(name):
            return ctx.enter_context(nc.semaphore(name))

        table = [nc.dram_tensor(f"table{k}", [NPAD, F], F32, kind="Internal").ap() for k in range(3)]
        scan_rows = [nc.dram_tensor(f"scan_rows{k}", [GROUPS * GE, F], F32, kind="Internal").ap() for k in range(3)]
        col_rows = [nc.dram_tensor(f"col_rows{k}", [FT * TC, F], F32, kind="Internal").ap() for k in range(2)]
        dst_rows = nc.dram_tensor("dst_rows", [CHUNKS // GC, GE], F32, kind="Internal").ap()
        sum_mask = nc.dram_tensor("sum_mask", [CHUNKS, P], BF16, kind="Internal").ap()
        max_mask = nc.dram_tensor("max_mask", [CHUNKS, P], BF16, kind="Internal").ap()
        col_mask = nc.dram_tensor("col_mask", [CHUNKS, WIN], BF16, kind="Internal").ap()

        EB = BLOCKS * P
        words = 9 * EB + 4 * GE + GE + 2 * HEADS + 5 * F
        second = 3 * TILES * F // 2 + TILES * DC // 2 + 2 * TG * F + 4 * P // 2 + 4 * (CELLS + CELLS % 2) // 2 \
            + 2 * PC + TC + TG * 6
        words = max(words, second)
        region = sb("region", [P, words])
        xin = sb("xin", [P, TILES, F])
        taken = [0]

        def part(shape, dt=F32):
            n = 1
            for d in shape[1:]:
                n *= d
            w = n * (2 if dt == BF16 else 4) // 4
            v = region[:, taken[0]:taken[0] + w]
            taken[0] += w
            v = v if dt == F32 else v.bitcast(dt)
            if len(shape) == 3:
                return v.rearrange("p (a b) -> p a b", b=shape[2])
            if len(shape) == 4:
                return v.rearrange("p (a b c) -> p a b c", b=shape[2], c=shape[3])
            return v

        src_i = part([P, BLOCKS, P], I32)
        dst_i = part([P, BLOCKS, P], I32)
        prev_i = part([P, BLOCKS, P], I32)
        src_f = part([P, BLOCKS, P])
        wgt_f = part([P, BLOCKS, P])
        dst_f = part([P, BLOCKS, P])
        off_f = part([P, BLOCKS, P])
        cell_f = part([P, BLOCKS, P])
        smask = part([P, BLOCKS, P], BF16)
        mmask = part([P, BLOCKS, P], BF16)
        level = part([P, 4, GE])
        level_junk = part([P, GE])
        sign_junk = part([P, 2, HEADS])
        wraw = part([P, 5, F])
        assert taken[0] <= words
        taken[0] = 0
        parts = part([P, 3, TILES, F], BF16)
        counts = [part([P, TILES, DC], BF16),
                  xin[:, :, :].rearrange("p t f -> p (t f)").bitcast(BF16)[:, 0:TILES * DC]
                  .rearrange("p (a c) -> p a c", c=DC)]
        rest = part([P, TG, F])
        hot_low = part([P, 4, P], BF16)
        hot_cell = part([P, 4, CELLS + CELLS % 2], BF16)
        hot_off = part([P, 2, POOL_CH, WIN])
        col_m = part([P, 2, TC], BF16)
        xn = part([P, TG, F])
        stats = part([P, TG, 6])
        assert taken[0] <= words

        src_t = sb("src_t", [P, EB], U32)
        wgt_t = sb("wgt_t", [P, EB])
        off_t = sb("off_t", [P, EB], BF16)
        low_t = sb("low_t", [P, EB], BF16)
        cell_t = sb("cell_t", [P, EB], BF16)
        span = sb("span", [P, BLOCKS])
        spanm = sb("spanm", [P, 1])
        spanr = sb("spanr", [1, 1])
        short_f = sb("short_f", [1, 1])
        short_i = sb("short_i", [1, 1], I32)
        short_p = sb("short_p", [P, 1])
        cmask = sb("cmask", [P, BLOCKS, WIN], BF16)
        cell_no = sb("cell_no", [P, CELL_BLOCKS, P], BF16)
        ident_b = sb("ident_b", [P, P], BF16)
        iota_f = sb("iota_f", [P, WIN])

        own = sb("own", [P, TILES, F])
        ids_i = sb("ids_i", [P, TILES], I32)
        ids = sb("ids", [P, TILES])
        idh = sb("idh", [P, TILES])
        signs = sb("signs", [P, TILES])
        head_row = sb("head_row", [P, TILES])
        head_idx = sb("head_idx", [P, TILES], U32)
        inner = sb("inner", [P, TILES])
        count = sb("count", [P, TILES + 1])
        indeg = sb("indeg", [P, TILES])
        deg = sb("deg", [P, TILES])
        sdeg = sb("sdeg", [P, TILES])
        dinv = sb("dinv", [P, TILES])
        has = sb("has", [P, TILES])
        h4 = sb("h4", [P, TILES, GC])
        le4 = sb("le4", [P, TILES, GC])
        nle = sb("nle", [P, TILES])
        first_dst = sb("first_dst", [P, TILES])
        pos = sb("pos", [P, TILES])
        posd = sb("posd", [P, TILES])
        last_f = sb("last_f", [P, TILES])
        last_i = sb("last_i", [P, TILES], I32)
        edge_i = sb("edge_i", [P, TILES], I32)
        chunk_i = sb("chunk_i", [P, TILES], I32)
        last_idx = sb("last_idx", [P, 2, TILES + 2 * TG], U32)
        own_flat = own[:, :, :].rearrange("p t f -> p (t f)")
        cell_no_i = own_flat[:, 2 * HEADS + 2:2 * HEADS + 2 + CELL_BLOCKS * P // 2].bitcast(I16)
        iota_i = own_flat[:, 4 * F * CELL_BLOCKS:4 * F * CELL_BLOCKS + WIN].bitcast(I32)
        heads_f = own_flat[0:1, 0:HEADS]
        heads_i = own_flat[0:1, HEADS:2 * HEADS].bitcast(I32)

        ident = sb("ident", [P, P])
        shift = sb("shift", [P, P])
        wrap = sb("wrap", [P, P])
        ones_row = sb("ones_row", [1, P])
        eps = sb("eps", [P, 1])
        wt = sb("wt", [P, 5, F])
        brow = sb("brow", [1, 4, F])
        bias = sb("bias", [P, 4, F])

        idx_win = sb("idx_win", [P, SLOTS, GC], U32)
        idx_turn = sb("idx_turn", [P, 2, POOL_CH], U32)
        got = sb("got", [P, SLOTS, GC, F])
        mask = sb("mask", [P, SLOTS, GE], BF16)
        scan = sb("scan", [P, 2, GE])
        rows = sb("rows", [P, SLOTS, GC, F])

        node_win = sb("node_win", [P, 2, TG], U32)
        node_got = got[:, :, :, :].rearrange("p s c f -> p (s c) f")[:, 0:2 * TG, :]\
            .rearrange("p (h t) f -> p h t f", h=2)
        agg = sb("agg", [P, TG, F])
        agg_t = sb("agg_t", [P, TG, F])
        res = sb("res", [P, TG, F])
        tab = sb("tab", [P, TG, F])
        mv = sb("mv", [P, TG, 2])
        sd = sb("sd", [P, TG])
        rstd = sb("rstd", [P, TG])

        bank_a = ps("bank_a", [P, 2, 512])
        bank_b = ps("bank_b", [P, 2, 512])
        bank_c = ps("bank_c", [P, 2, 512])
        bank_d = ps("bank_d", [P, 2, 512])

        def tiles(bank):
            return bank[:, :, :].rearrange("p a b -> p (a b)")[:, 0:TG * F].rearrange("p (t f) -> p t f", t=TG)

        na, nb, ncc, nd = tiles(bank_a), tiles(bank_b), tiles(bank_c), tiles(bank_d)

        edge_clear = sem("edge_clear")
        dst_loaded = sem("dst_loaded")
        prev_loaded = sem("prev_loaded")
        src_loaded = sem("src_loaded")
        wgt_loaded = sem("wgt_loaded")
        heads_loaded = sem("heads_loaded")
        par_loaded = sem("par_loaded")
        x_loaded = sem("x_loaded")
        x_clear = sem("x_clear")
        ids_made = sem("ids_made")
        const_made = sem("const_made")
        dst_cast = sem("dst_cast")
        masks_made = sem("masks_made")
        dst_stored = sem("dst_stored")
        masks_stored = sem("masks_stored")
        heads_cast = sem("heads_cast")
        heads_spread = sem("heads_spread")
        idh_made = sem("idh_made")
        counted = sem("counted")
        rows_found = sem("rows_found")
        level_got = [sem(f"level_got{k}") for k in range(4)]
        level_done = sem("level_done")
        count_done = sem("count_done")
        shifted = sem("shifted")
        deg_step = sem("deg_step")
        deg_done = sem("deg_done")
        root_done = sem("root_done")
        dinv_done = sem("dinv_done")
        z_even = sem("z_even")
        z_odd = sem("z_odd")
        z_stored = sem("z_stored")
        src_cast = sem("src_cast")
        flipped = sem("flipped")
        flip_copied = sem("flip_copied")
        flip_kept = sem("flip_kept")
        bias_spread = sem("bias_spread")
        bias_kept = sem("bias_kept")
        prep = sem("prep")
        span_turned = sem("span_turned")
        short_spread = sem("short_spread")
        short_known = sem("short_known")
        iota_made = sem("iota_made")
        iota_spread = sem("iota_spread")
        idx_step = sem("idx_step")
        own_done = sem("own_done")

        WINDOWS = TURNS + 2
        passed = {mybir.EngineType.Pool: sem("pool_passed"), mybir.EngineType.DVE: sem("dve_passed")}
        def sems(name, n):
            return [sem(f"{name}{k}") for k in range(n)]

        win_ready = sems("win_ready", 3)
        gathered = [sems(f"gathered{k}_", SLOTS) for k in range(3)]
        scaled = sem("scaled")
        turned = sems("turned", 3)
        mask_here = [sems(f"mask_here{k}_", SLOTS) for k in range(3)]
        scanned = sems("scanned", 3)
        turned_back = sems("turned_back", 3)
        rows_ready = sems("rows_ready", 3)
        stored = [sems(f"stored{k}_", SLOTS) for k in range(3)]
        hot_ready = sems("hot_ready", 2)
        off_ready = sems("off_ready", 2)
        built = sems("built", 2)
        kept = sems("kept", 2)
        applied = sems("applied", 2)
        part_hi = sems("part_hi", 2)
        rest_hi = sems("rest_hi", 2)
        part_mid = sems("part_mid", 2)
        parts_done = sems("parts_done", 2)

        node_win_ready = sem("node_win_ready")
        node_gathered = sems("node_gathered", 2)
        agg_made = sem("agg_made")
        agg_pre = sem("agg_pre")
        agg_turned = sem("agg_turned")
        agg_t_copied = sem("agg_t_copied")
        linear_done = sem("linear_done")
        res_made = sem("res_made")
        res_pre = sem("res_pre")
        stats_made = sem("stats_made")
        mv_made = sem("mv_made")
        sd_made = sem("sd_made")
        rstd_made = sem("rstd_made")
        normed = sem("normed")
        x1_kept = sem("x1_kept")
        x1_turned = sem("x1_turned")
        x1_t_copied = sem("x1_t_copied")
        table_out = sem("table_out")
        half_out = sem("half_out")
        tab_ready = sem("tab_ready")
        half_kept = sem("half_kept")
        half_biased = sem("half_biased")
        tab_stored = sem("tab_stored")

        def wait(eng, s, n):
            if not isinstance(n, int) or n > 0:
                eng.wait_ge(s, n)

        def wait_alone(eng, s, n):
            wait(eng, s, n)
            eng.sem_inc(passed[eng.engine], 1)

        def turns(eng, n, body):
            body(0, True, False)
            with eng.Fori(1, n - 1) as i:
                body(i, False, False)
            body(n - 1, False, True)

        def turn_pairs(eng, body):
            for i in range(4):
                body(i, i % 2, i // 2, i < 2)
            with eng.Fori(2, FT // 2) as n:
                body(2 * n, 0, n, False)
                body(2 * n + 1, 1, n, False)
            body(FT - 1, 0, FT // 2, False)

        def unit(s, h, pair):
            return (h * UNITS + s) % SLOTS, 2 * UNITS // SLOTS * pair + (h * UNITS + s) // SLOTS

        def node_steps(eng, front, back):
            front(0, 0, 0)
            front(1, 1, 0)
            back(0, 0, 0)
            front(2, 0, 1)
            back(1, 1, 0)
            with eng.Fori(1, TURNS // 2) as m:
                front(2 * m + 1, 1, m)
                back(2 * m, 0, m)
                front(2 * m + 2, 0, m + 1)
                back(2 * m + 1, 1, m)
            back(TURNS - 1, 0, TURNS // 2)

        def ways(eng, k, short, general):
            if k == 2:
                general()
                return
            if k == 0:
                eng.wait_ge(short_known, 1)
            go = eng.value_load(short_i[0:1, 0:1], min_val=0, max_val=1)
            with eng.If(go == 1):
                short()
            with eng.Else():
                general()

        def blocks_of(dram, tile):
            return dram.rearrange("(b p) j -> p b j", p=P), tile

        def load_edges(sp, arr, tile, done):
            sp.dma_start(tile[:, 0:BLOCKS - 1, :],
                         arr[0:FULL].rearrange("(b p j) -> p b j", p=P, j=P)).then_inc(done, 16)
            sp.dma_start(tile[0:ROWS_LEFT, BLOCKS - 1, :],
                         arr[FULL:FULL + ROWS_LEFT * P].rearrange("(p j) -> p j", j=P)).then_inc(done, 16)
            sp.dma_start(tile[ROWS_LEFT:ROWS_LEFT + 1, BLOCKS - 1, 0:EDGES_LEFT],
                         arr[FULL + ROWS_LEFT * P:EDGES].rearrange("(p j) -> p j", p=1)).then_inc(done, 16)

        def load_x(sp):
            sp.dma_start(xin[:, 0:TILES - 1, :],
                         x[0:(TILES - 1) * P, :].rearrange("(t p) f -> p t f", p=P)).then_inc(x_loaded, 16)
            sp.dma_start(xin[0:TAIL, TILES - 1, :], x[(TILES - 1) * P:NODES, :]).then_inc(x_loaded, 16)

        def one(tile, t):
            return tile[:, bass.ds(t, 1), :].rearrange("p a f -> p (a f)")

        flips = [(kind, t, b, to[:, b * P:(b + 1) * P])
                 for kind, t, to in (("src", src_f, src_t), ("off", off_f, off_t), ("low", src_f, low_t),
                                     ("cell", cell_f, cell_t), ("wgt", wgt_f, wgt_t)) for b in range(BLOCKS)]
        flips += [("par", wraw, b, wt[:, b, :]) for b in range(5)]
        SPAN_STEP, LOW_STEP, CELL_STEP, PREP = 4, 6, 9, 13
        FLIPPED = len(flips)
        flip_needs = {"src": (src_cast, 1), "off": (prep, 1), "low": (prep, LOW_STEP), "cell": (prep, CELL_STEP),
                      "wgt": (wgt_loaded, 48), "par": (par_loaded, 9 * 16)}
        build = [b[:, h, 0:CELLS] for b, h in ((bank_c, 0), (bank_c, 1))]
        iota = bank_d[:, 0, :].bitcast(BF16)[:, 0:CELLS]

        block = ctx.enter_context(nc.Block())

        @block.sync
        def _(sp):
            with nc.allow_non_contiguous_dma(reason="one destination per group, 403 in all"):
                sp.dma_start(heads_i[0:1, :], dst[0:(HEADS - 1) * GE + 1:GE].rearrange("(a n) -> a n", a=1))\
                  .then_inc(heads_loaded, 16)
            sp.wait_ge(edge_clear, 1)
            load_edges(sp, dst, dst_i, dst_loaded)
            load_edges(sp, src, src_i, src_loaded)
            sp.wait_ge(dst_cast, 1)
            flat = dst_rows.rearrange("g e -> (g e)").rearrange("(c j) -> c j", j=P)
            sp.dma_start(*blocks_of(flat, dst_f)).then_inc(dst_stored, 16)
            sp.dma_start(prev_i[0:1, 0, 1:P], dst[0:P - 1].rearrange("(p j) -> p j", p=1)).then_inc(prev_loaded, 16)
            sp.dma_start(prev_i[1:P, 0, :], dst[P - 1:P * P - 1].rearrange("(p j) -> p j", j=P))\
              .then_inc(prev_loaded, 16)
            sp.dma_start(prev_i[:, 1:BLOCKS - 1, :],
                         dst[P * P - 1:FULL - 1].rearrange("(b p j) -> p b j", p=P, j=P)).then_inc(prev_loaded, 16)
            sp.dma_start(prev_i[0:ROWS_LEFT, BLOCKS - 1, :],
                         dst[FULL - 1:FULL + ROWS_LEFT * P - 1].rearrange("(p j) -> p j", j=P))\
              .then_inc(prev_loaded, 16)
            sp.dma_start(prev_i[ROWS_LEFT:ROWS_LEFT + 1, BLOCKS - 1, 0:EDGES_LEFT],
                         dst[FULL + ROWS_LEFT * P - 1:EDGES - 1].rearrange("(p j) -> p j", p=1))\
              .then_inc(prev_loaded, 16)
            load_edges(sp, edge_weight, wgt_f, wgt_loaded)
            for k, w in enumerate((w1, w2, pool_w, final_w[:, 0:F], final_w[:, F:2 * F])):
                sp.dma_start(wraw[:, k, :], w).then_inc(par_loaded, 16)
            for k, b in enumerate((b1, b2, final_b, pool_b)):
                sp.dma_start(brow[0:1, k, :], b.rearrange("(a f) -> a f", a=1)).then_inc(par_loaded, 16)
            sp.wait_ge(x_clear, 1)
            load_x(sp)
            sp.wait_ge(masks_made, 3)
            sp.dma_start(*blocks_of(sum_mask, smask)).then_inc(masks_stored, 16)
            sp.dma_start(*blocks_of(max_mask, mmask)).then_inc(masks_stored, 16)
            sp.dma_start(*blocks_of(col_mask, cmask[:, :, :])).then_inc(masks_stored, 16)
            for a, b in ((0, Z_PART), (Z_PART, TILES)):
                sp.wait_ge(z_even, (b + 1) // 2)
                sp.wait_ge(z_odd, b // 2)
                sp.dma_start(table[0].rearrange("(t p) f -> p t f", p=P)[:, a:b, :], own[:, a:b, :])\
                  .then_inc(z_stored, 16)
            sp.wait_ge(masks_stored, 48)

            for k in range(3):
                def short():
                    m = col_mask.rearrange("c j -> (c j)").rearrange("(a e) -> a e", a=1)

                    def turn(i, h, pair, first):
                        wait(sp, scanned[k], 2 * (i - 1))
                        sp.dma_start(col_m[:, h, :], m[0:1, bass.ds(i * TC, TC)].to_broadcast([P, TC]))\
                          .then_inc(mask_here[k][h], 16)
                        if not first:
                            store(i - 2, h)

                    def store(i, h):
                        sp.wait_ge(rows_ready[k], i + 1)
                        whole = (len(BACK) - 1) * P
                        sp.dma_start(col_rows[k][bass.ds(i * TC, whole), :].rearrange("(b p) f -> p b f", p=P),
                                     rows[:, h, 0:len(BACK) - 1, :]).then_inc(stored[k][h], 16)
                        sp.dma_start(col_rows[k][bass.ds(i * TC + whole, BACK[-1]), :],
                                     rows[0:BACK[-1], h, len(BACK) - 1, :]).then_inc(stored[k][h], 16)

                    turn_pairs(sp, turn)
                    store(FT - 2, 1)
                    store(FT - 1, 0)

                def general():
                    m = (sum_mask, sum_mask, max_mask)[k].rearrange("c j -> (c j)").rearrange("(a e) -> a e", a=1)
                    out_rows = scan_rows[k].rearrange("(g p c) f -> p g (c f)", p=P, c=GC)

                    def load_mask(g, s):
                        sp.dma_start(mask[:, s, :], m[0:1, bass.ds(g * GE, GE)].to_broadcast([P, GE]))\
                          .then_inc(mask_here[k][s], 16)

                    for s in range(SLOTS - 1):
                        load_mask(s, s)

                    def body(i, first, last):
                        for s in range(SLOTS):
                            g = i * SLOTS + s
                            if not (last and s > 0):
                                wait(sp, scanned[k], g)
                                load_mask(g + SLOTS - 1, (s + SLOTS - 1) % SLOTS)
                            sp.wait_ge(rows_ready[k], g + 1)
                            sp.dma_start(out_rows[:, bass.ds(g, 1), :].rearrange("p g e -> p (g e)"),
                                         rows[:, s, :, :].rearrange("p c f -> p (c f)"))\
                              .then_inc(stored[k][s], 16)

                    turns(sp, ROUNDS, body)

                ways(sp, k, short, general)
                if k == 1:
                    load_x(sp)

                def node(i, first, last):
                    sp.wait_ge(tab_ready, i + k * TURNS + 1)
                    if k < 2:
                        sp.dma_start(table[k + 1].rearrange("(t p) f -> p t f", p=P)[:, bass.ds(i * TG, TG), :],
                                     tab[:, :, :]).then_inc(tab_stored, 16)
                    elif not last:
                        sp.dma_start(out[0:(TILES - 1) * P, :].rearrange("(t p) f -> p t f", p=P)
                                     [:, bass.ds(i * TG, TG), :], tab[:, :, :]).then_inc(tab_stored, 16)
                    else:
                        sp.dma_start(out[i * TG * P:(TILES - 1) * P, :].rearrange("(t p) f -> p t f", p=P),
                                     tab[:, 0:TG - 1, :]).then_inc(tab_stored, 16)
                        sp.dma_start(out[(TILES - 1) * P:NODES, :], tab[0:TAIL, TG - 1, :])\
                          .then_inc(tab_stored, 16)

                turns(sp, TURNS, node)
            sp.wait_ge(tab_stored, 16 * (3 * TURNS + 1))

        @block.gpsimd
        def _(pool):
            nc.gpsimd.iota(ids_i[:, :], pattern=[[P, TILES]], base=0, channel_multiplier=1).then_inc(ids_made, 1)
            nc.gpsimd.memset(dst_i[:, BLOCKS - 1, :], int(NOWHERE))
            nc.gpsimd.memset(prev_i[:, 0, :], -1)
            nc.gpsimd.memset(prev_i[:, BLOCKS - 1, :], -1)
            nc.gpsimd.memset(src_i[:, BLOCKS - 1, :], 0)
            nc.gpsimd.memset(wgt_f[:, BLOCKS - 1, :], 0.0).then_inc(edge_clear, 1)
            for t, base in ((ident, 0), (shift, 1), (wrap, 1 - P)):
                nc.gpsimd.memset(t[:, :], 0.0).then_inc(const_made, 1)
            pool.wait_ge(const_made, 3)
            for t, base in ((ident, 0), (shift, 1), (wrap, 1 - P)):
                nc.gpsimd.affine_select(out=t[:, :], in_=t[:, :], compare_op=ALU.not_equal, fill=1.0, base=base,
                                        pattern=[[-1, P]], channel_multiplier=1).then_inc(const_made, 1)
            nc.gpsimd.memset(ones_row[:, :], 1.0).then_inc(const_made, 1)
            nc.gpsimd.memset(eps[:, :], EPS).then_inc(const_made, 1)
            nc.gpsimd.memset(xin[:, TILES - 1, :], 0.0).then_inc(x_clear, 1)
            nc.gpsimd.iota(cell_no_i, pattern=[[P, CELL_BLOCKS], [0, P]], base=-MID, channel_multiplier=1)
            nc.gpsimd.iota(iota_i, pattern=[[1, WIN]], base=0, channel_multiplier=0)\
              .then_inc(iota_made, 1)

            pool.wait_ge(dst_stored, 16)
            for t in range(TILES):
                pool.wait_ge(rows_found, t // TG + 1)
                if t >= 4:
                    pool.wait_ge(level_done, t - 3)
                nc.gpsimd.indirect_dma_start(level[:, t % 4, :], None, dst_rows[:, :],
                                             bass.IndirectOffsetOnAxis(ap=head_idx[:, t:t + 1], axis=0))\
                  .then_inc(level_got[t % 4], 16)

            for k in range(3):
                if k == 0:
                    pool.wait_ge(z_stored, 32)
                else:
                    pool.wait_ge(tab_stored, 16 * k * TURNS)

                def gather_nodes(from_rows):
                    def group(i, h, m):
                        pool.wait_ge(node_win_ready, k * WINDOWS + i + 1)
                        wait_alone(pool, agg_made, i + k * TURNS - 1)
                        for j in range(TG):
                            nc.gpsimd.indirect_dma_start(
                                node_got[:, h, j, :], None, from_rows[:, :],
                                bass.IndirectOffsetOnAxis(ap=node_win[:, h, j:j + 1], axis=0))\
                              .then_inc(node_gathered[h], 16)

                    node_steps(pool, group, lambda i, h, m: None)

                def fill(s, window):
                    for c in range(GC):
                        nc.gpsimd.indirect_dma_start(
                            got[:, s, c, :], None, table[k][:, :],
                            bass.IndirectOffsetOnAxis(ap=window[:, c:c + 1], axis=0))\
                          .then_inc(gathered[k][s], 16)

                def short():
                    def turn(i, h, pair, first):
                        pool.wait_ge(win_ready[k], i + 1)
                        for s in range(UNITS):
                            wait_alone(pool, turned[k], i * UNITS + s - SLOTS + 1)
                            fill(unit(s, h, pair)[0], idx_turn[:, h, s * GC:(s + 1) * GC])

                    turn_pairs(pool, turn)
                    for h in range(2):
                        pool.wait_ge(stored[k][h], 32 * ((FT + 1 - h) // 2))
                    gather_nodes(col_rows[k])

                def general():
                    def body(i, first, last):
                        for s in range(SLOTS):
                            g = i * SLOTS + s
                            pool.wait_ge(win_ready[k], g + 1)
                            wait_alone(pool, turned[k], g - SLOTS + 1)
                            fill(s, idx_win[:, s, :])

                    turns(pool, ROUNDS, body)
                    for s in range(SLOTS):
                        pool.wait_ge(stored[k][s], 16 * ROUNDS)
                    gather_nodes(scan_rows[k])

                ways(pool, k, short, general)

        @block.scalar
        def _(act):
            act.wait_ge(heads_spread, 1)
            act.wait_ge(idh_made, 1)
            for t in range(TILES):
                if t >= 2:
                    act.wait_ge(counted, t - 1)
                nc.scalar.activation(sign_junk[:, t % 2, :], bank_d[:, 0, 0:HEADS], ACT.Sign, scale=-1.0,
                                     bias=idh[:, t:t + 1], accum_out=signs[:, t:t + 1]).then_inc(counted, 1)
            for n in range(BLOCKS, FLIPPED):
                act.wait_ge(flipped, n + 1)
                nc.scalar.copy(flips[n][3], bank_a[:, n % 2, 0:P]).then_inc(flip_kept, 1)
            act.wait_ge(deg_done, 1)
            nc.scalar.activation(sdeg[:, :], deg[:, :], ACT.Sqrt).then_inc(root_done, 1)
            act.wait_ge(dinv_done, 1)
            act.wait_ge(x_loaded, 32)
            for t in range(0, TILES, 2):
                nc.scalar.activation(own[:, t, :], xin[:, t, :], ACT.Copy, scale=dinv[:, t:t + 1])\
                  .then_inc(z_even, 1)

            for k in range(3):
                def short():
                    act.wait_ge(z_even, (TILES + 1) // 2)
                    act.wait_ge(z_odd, TILES // 2)
                    if k == 0:
                        act.wait_ge(masks_stored, 48)
                        act.wait_ge(prep, PREP)
                        act.wait_ge(flip_copied, BLOCKS)
                        act.wait_ge(flip_kept, FLIPPED - BLOCKS)

                    def table_parts(j):
                        n, step = j // 4, j % 4
                        g = slice(n * TG, (n + 1) * TG)
                        if n < TURNS and step == 0:
                            nc.scalar.copy(parts[:, 0, g, :], own[:, g, :]).then_inc(part_hi[k], 1)
                        if n < TURNS and step == 2:
                            act.wait_ge(rest_hi[k], n + 1)
                            nc.scalar.copy(parts[:, 1, g, :], rest[:, :, :]).then_inc(part_mid[k], 1)

                    def keep_rows(i, h, pair):
                        act.wait_ge(turned_back[k], i + 1)
                        wait(act, stored[k][h], 32 * pair)
                        whole = (len(BACK) - 1) * P
                        nc.scalar.copy(rows[:, h, 0:len(BACK) - 1, :],
                                       bank_b[:, 0, 0:whole].rearrange("p (b f) -> p b f", f=P))
                        nc.scalar.copy(rows[0:BACK[-1], h, len(BACK) - 1, :], bank_b[0:BACK[-1], 0, whole:whole + P])\
                           .then_inc(rows_ready[k], 1)

                    def turn(i, h, pair, first):
                        for j in range(DENSE_CH):
                            act.wait_ge(built[k], i * DENSE_CH + j + 1)
                            if j == 0:
                                wait(act, applied[k], i - 1)
                            nc.scalar.copy(counts[h][:, :, j * WIN:(j + 1) * WIN],
                                           build[j % 2].rearrange("p (a l) -> p a l", l=WIN)).then_inc(kept[k], 1)
                            if isinstance(i, int) and i == 0:
                                table_parts(j)
                            if j == 24 and not first:
                                keep_rows(i - 2, h, pair - 1)

                    turn_pairs(act, turn)
                    keep_rows(FT - 2, 1, FT // 2 - 1)
                    keep_rows(FT - 1, 0, FT // 2)

                def general():
                    def keep_rows(b, g, uses):
                        act.wait_ge(turned_back[k], g + 1)
                        wait(act, stored[k][b], uses * 16)
                        nc.scalar.copy(rows[:, b, :, :], bank_b[:, b % 2, :].rearrange("p (c f) -> p c f", c=GC))\
                           .then_inc(rows_ready[k], 1)

                    def body(i, first, last):
                        for s in range(SLOTS):
                            g = i * SLOTS + s
                            if k == 2:
                                act.wait_ge(gathered[k][s], (i + 1) * 16 * GC)
                                for c in range(GC):
                                    a = nc.scalar.activation(got[:, s, c, :], got[:, s, c, :], ACT.Copy,
                                                             scale=wgt_t[:, bass.ds(g * GC + c, 1)])
                                a.then_inc(scaled, 1)
                            if s > 0 or not first:
                                keep_rows((s - 1) % SLOTS, g - 1, i - (1 if s == 0 else 0))

                    turns(act, ROUNDS, body)
                    keep_rows(SLOTS - 1, GROUPS - 1, ROUNDS - 1)

                ways(act, k, short, general)

                def front(i, h, m):
                    n = i + k * TURNS
                    act.wait_ge(agg_turned, n + 1)
                    nc.scalar.copy(agg_t[:, :, :], na).then_inc(agg_t_copied, 1)

                def back(i, h, m):
                    n = i + k * TURNS
                    group = slice(None), bass.ds(i * TG, TG), slice(None)
                    if k == 0:
                        act.wait_ge(tab_ready, n + 1)
                        nc.scalar.copy(own[group], tab[:, :, :]).then_inc(own_done, 1)
                        return
                    act.wait_ge(mv_made, (n - TURNS + 1) * TG)
                    nc.scalar.activation(sd[:, :], mv[:, :, 1], ACT.Sqrt, bias=eps[:, 0:1]).then_inc(sd_made, 1)
                    if k == 1:
                        act.wait_ge(normed, i + 1)
                        nc.scalar.copy(xin[group], xn[:, :, :]).then_inc(x1_kept, 1)
                        act.wait_ge(x1_turned, i + 1)
                        nc.scalar.copy(agg_t[:, :, :], nd).then_inc(x1_t_copied, 1)
                        act.wait_ge(table_out, i + 1)
                        wait(act, tab_stored, 16 * n)
                        nc.scalar.copy(tab[:, :, :], ncc).then_inc(tab_ready, 1)
                        act.wait_ge(half_out, i + 1)
                        nc.scalar.copy(own[group], nd).then_inc(half_kept, 1)

                node_steps(act, front, back)

        @block.tensor
        def _(pe):
            pe.wait_ge(const_made, 8)
            pe.wait_ge(heads_cast, 1)
            nc.tensor.matmul(bank_d[:, 0, 0:HEADS], ones_row[:, :], heads_f[:, :], start=True, stop=True)\
              .then_inc(heads_spread, 1)
            for n, (kind, t, b, _) in enumerate(flips):
                if b == 0:
                    pe.wait_ge(*flip_needs[kind])
                if n - 2 >= BLOCKS:
                    pe.wait_ge(flip_kept, n - 1 - BLOCKS)
                elif n >= 2:
                    pe.wait_ge(flip_copied, n - 1)
                nc.tensor.transpose(bank_a[:, n % 2, 0:P], t[:, b, :], ident[:, :]).then_inc(flipped, 1)
            pe.wait_ge(par_loaded, 9 * 16)
            nc.tensor.matmul(bank_c[:, 0, :], ones_row[:, :], brow[0:1, :, :].rearrange("a k f -> a (k f)"),
                             start=True, stop=True).then_inc(bias_spread, 1)
            pe.wait_ge(prep, SPAN_STEP)
            nc.tensor.transpose(bank_c[0:1, 1, 0:P], spanm[:, 0:1], ident[:, :]).then_inc(span_turned, 1)
            pe.wait_ge(short_known, 1)
            nc.tensor.matmul(bank_c[:, 1, P:P + 1], ones_row[:, :], short_f[:, :], start=True, stop=True)\
              .then_inc(short_spread, 1)
            pe.wait_ge(count_done, 2)
            nc.tensor.matmul(bank_b[:, 0, 0:TILES], shift[:, :], count[:, 1:TILES + 1], start=True, stop=False)
            nc.tensor.matmul(bank_b[:, 0, 0:TILES], wrap[:, :], count[:, 0:TILES], start=False, stop=True)\
              .then_inc(shifted, 1)
            pe.wait_ge(deg_done, 1)
            pe.wait_ge(bias_kept, 1)
            pe.wait_ge(idx_step, 1)
            pe.wait_ge(flip_copied, BLOCKS)
            pe.wait_ge(flip_kept, FLIPPED - BLOCKS)

            for k in range(3):
                def short():
                    def apply(i, h, n, pieces):
                        if n == 0:
                            pe.wait_ge(kept[k], (i + 1) * DENSE_CH)
                            wait(pe, scanned[k], 2 * (i - 1))
                            pe.wait_ge(parts_done[k], TURNS)
                        lo, hi = TILES * n // pieces, TILES * (n + 1) // pieces
                        for a in range(lo, hi):
                            for q in range(3):
                                mm = nc.tensor.matmul(bank_a[:, h, 0:DC], parts[:, q, a, :],
                                                      counts[h][:, a, :], start=(a == 0 and q == 0),
                                                      stop=(a == TILES - 1 and q == 2))
                        if n == pieces - 1:
                            mm.then_inc(applied[k], 1)

                    def products(i, h, pair, s):
                        wait(pe, scanned[k], 2 * i - 1)
                        slot, uses = unit(s, h, pair)
                        pe.wait_ge(gathered[k][slot], (uses + 1) * 16 * GC)
                        pe.wait_ge(off_ready[k], i + 1)
                        for c in range(s * GC, (s + 1) * GC):
                            mm = nc.tensor.matmul(bank_d[:, 1, c * WIN:(c + 1) * WIN], got[:, slot, c % GC, :],
                                                  hot_off[:, h, c, :], start=True, stop=True)
                        mm.then_inc(turned[k], 1)

                    def rows_back(i, h):
                        pe.wait_ge(scanned[k], 2 * i + 2)
                        wait(pe, rows_ready[k], i)
                        for b, n in enumerate(BACK):
                            mm = nc.tensor.transpose(bank_b[0:n, 0, b * P:(b + 1) * P], scan[:, h, b * P:b * P + n],
                                                     ident[:, :])
                        mm.then_inc(turned_back[k], 1)

                    def turn(i, h, pair, first):
                        for j in range(DENSE_CH):
                            pe.wait_ge(hot_ready[k], i * DENSE_CH + j + 1)
                            wait(pe, kept[k], i * DENSE_CH + j - 1)
                            nc.tensor.matmul(build[j % 2], hot_low[:, j % 4, :], hot_cell[:, j % 4, 0:CELLS],
                                             start=True, stop=True).then_inc(built[k], 1)
                            if not (first and h == 0):
                                apply(i - 1, 1 - h, j, DENSE_CH)
                            if j in PRODUCTS_AT:
                                products(i, h, pair, PRODUCTS_AT.index(j))
                            if j == 20 and not first:
                                rows_back(i - 2, h)

                    for b in range(CELL_BLOCKS):
                        n = min(P, CELLS - b * P)
                        mm = nc.tensor.transpose(iota[:, b * P:b * P + n], cell_no[0:n, b, :], ident_b[0:n, 0:n])
                    mm.then_inc(iota_spread, 1)
                    turn_pairs(pe, turn)
                    for n in range(DENSE_CH):
                        apply(FT - 1, 0, n, DENSE_CH)
                    rows_back(FT - 2, 1)
                    rows_back(FT - 1, 0)
                    pe.wait_ge(rows_ready[k], FT)

                def general():
                    def back(n, q):
                        pe.wait_ge(scanned[k], n + 1)
                        wait(pe, rows_ready[k], n - 1)
                        for c in range(GC):
                            a = nc.tensor.transpose(bank_b[:, q, c * P:(c + 1) * P], scan[:, q, c * P:(c + 1) * P],
                                                    ident[:, :])
                        a.then_inc(turned_back[k], 1)

                    def body(i, first, last):
                        for s in range(SLOTS):
                            g = i * SLOTS + s
                            if k == 2:
                                pe.wait_ge(scaled, g + 1)
                            else:
                                pe.wait_ge(gathered[k][s], (i + 1) * 16 * GC)
                            wait(pe, scanned[k], g - 1)
                            for c in range(GC):
                                a = nc.tensor.transpose(bank_a[:, s % 2, c * P:(c + 1) * P], got[:, s, c, :],
                                                        ident[:, :])
                            a.then_inc(turned[k], 1)
                            if s > 0 or not first:
                                back(g - 1, (s - 1) % 2)

                    turns(pe, ROUNDS, body)
                    back(GROUPS - 1, (SLOTS - 1) % 2)
                    pe.wait_ge(rows_ready[k], GROUPS)

                ways(pe, k, short, general)

                def front(i, h, m):
                    n = i + k * TURNS
                    pe.wait_ge(agg_made, n + 1)
                    wait(pe, agg_t_copied, n)
                    for j in range(TG):
                        a = nc.tensor.transpose(na[:, j, :], agg[:, j, :], ident[:, :])
                    a.then_inc(agg_turned, 1)
                    pe.wait_ge(agg_t_copied, n + 1)
                    wait(pe, res_made, n)
                    for j in range(TG):
                        a = nc.tensor.matmul(nb[:, j, :], agg_t[:, j, :], wt[:, (0, 1, 4)[k], :],
                                             start=True, stop=True)
                    a.then_inc(linear_done, 1)

                def back(i, h, m):
                    if k != 1:
                        return
                    pe.wait_ge(normed, i + 1)
                    wait(pe, half_kept, i)
                    for j in range(TG):
                        a = nc.tensor.transpose(nd[:, j, :], xn[:, j, :], ident[:, :])
                    a.then_inc(x1_turned, 1)
                    pe.wait_ge(x1_t_copied, i + 1)
                    pe.wait_ge(tab_ready, i + TURNS)
                    for j in range(TG):
                        a = nc.tensor.matmul(ncc[:, j, :], agg_t[:, j, :], wt[:, 2, :], start=True, stop=True)
                    a.then_inc(table_out, 1)
                    for j in range(TG):
                        a = nc.tensor.matmul(nd[:, j, :], agg_t[:, j, :], wt[:, 3, :], start=True, stop=True)
                    a.then_inc(half_out, 1)

                node_steps(pe, front, back)

        @block.vector
        def _(dve):
            steps = [0]

            def step(ins):
                ins.then_inc(prep, 1)
                steps[0] += 1
                dve.wait_ge(prep, steps[0])

            dve.wait_ge(heads_loaded, 16)
            nc.vector.tensor_copy(heads_f[:, :], heads_i[:, :]).then_inc(heads_cast, 1)
            dve.wait_ge(ids_made, 1)
            nc.vector.tensor_copy(ids[:, :], ids_i[:, :]).then_inc(ids_made, 1)
            dve.wait_ge(ids_made, 2)
            nc.vector.tensor_scalar(idh[:, :], ids[:, :], 0.5, None, ALU.add).then_inc(idh_made, 1)
            nc.vector.memset(count[:, 0:1], 0.0).then_inc(count_done, 1)
            dve.wait_ge(dst_loaded, 48)
            nc.vector.tensor_copy(dst_f[:, :, :], dst_i[:, :, :]).then_inc(dst_cast, 1)
            dve.wait_ge(src_loaded, 48)
            nc.vector.tensor_copy(src_f[:, :, :], src_i[:, :, :]).then_inc(src_cast, 1)

            def prepare_offsets():
                dve.wait_ge(dst_cast, 1)
                step(nc.vector.tensor_tensor(off_f[:, :, :], dst_f[:, :, :],
                                             dst_f[:, :, 0:1].to_broadcast([P, BLOCKS, P]), ALU.subtract))

            def prepare_masks():
                dve.wait_ge(prev_loaded, 80)
                nc.vector.tensor_tensor(smask[:, :, :], dst_i[:, :, :], prev_i[:, :, :], ALU.is_equal)\
                  .then_inc(masks_made, 1)

            def prepare_max_mask():
                dve.wait_ge(masks_made, 1)
                nc.vector.tensor_scalar(mmask[:, :, :], smask[:, :, :], 1.0, -RESET, ALU.subtract, ALU.mult)\
                  .then_inc(masks_made, 1)

            def prepare_span():
                step(nc.vector.scalar_tensor_tensor(out=cell_f[:, :, :], in0=dst_f[:, :, :], scalar=NOWHERE,
                                                    in1=off_f[:, :, :], op0=ALU.is_lt, op1=ALU.mult))
                step(nc.vector.tensor_reduce(span[:, :], cell_f[:, :, :], AX.X, ALU.max))
                step(nc.vector.tensor_reduce(spanm[:, :], span[:, :], AX.X, ALU.max))

            def prepare_low():
                dve.wait_ge(masks_made, 1)
                step(nc.vector.tensor_scalar(prev_i[:, :, :], src_i[:, :, :], P - 1, None, ALU.bitwise_and))
                dve.wait_ge(flip_copied, BLOCKS)
                step(nc.vector.tensor_copy(src_f[:, :, :], prev_i[:, :, :]))

            def prepare_cell():
                step(nc.vector.tensor_tensor(src_i[:, :, :], src_i[:, :, :], prev_i[:, :, :], ALU.subtract))
                step(nc.vector.scalar_tensor_tensor(out=cell_f[:, :, :], in0=src_i[:, :, :], scalar=WIN / P,
                                                    in1=off_f[:, :, :], op0=ALU.mult, op1=ALU.add))
                step(nc.vector.tensor_scalar(cell_f[:, :, :], cell_f[:, :, :], -float(MID), None, ALU.add))

            def prepare_way():
                dve.wait_ge(span_turned, 1)
                step(nc.vector.tensor_reduce(spanr[:, :], bank_c[0:1, 1, 0:P], AX.X, ALU.max))
                step(nc.vector.tensor_scalar(short_f[:, :], spanr[:, :], WIN - 0.5, None, ALU.is_lt))
                nc.vector.tensor_copy(short_i[:, :], short_f[:, :]).then_inc(short_known, 1)

            def prepare_columns():
                dve.wait_ge(iota_made, 1)
                dve.wait_ge(const_made, 8)
                nc.vector.tensor_copy(cell_no[:, :, :], cell_no_i.rearrange("p (b c) -> p b c", c=P))
                nc.vector.tensor_copy(ident_b[:, :], ident[:, :])
                step(nc.vector.tensor_copy(iota_f[:, :], iota_i))
                step(nc.vector.tensor_tensor(cmask[:, :, :],
                                             iota_f[:, :].rearrange("p (a l) -> p a l", a=1)
                                             .to_broadcast([P, BLOCKS, WIN]),
                                             span[:, :].rearrange("p (b l) -> p b l", l=1)
                                             .to_broadcast([P, BLOCKS, WIN]), ALU.is_gt))
                nc.vector.tensor_copy(cmask[:, :, 0:1], smask[:, :, 0:1]).then_inc(masks_made, 1)

            def take(n):
                kind, _, b, to = flips[n]
                dve.wait_ge(flipped, n + 1)
                nc.vector.tensor_copy(to, bank_a[:, n % 2, 0:P]).then_inc(flip_copied, 1)

            def find_rows(n):
                g = slice(n * TG, (n + 1) * TG)
                dve.wait_ge(counted, (n + 1) * TG)
                nc.vector.tensor_scalar(head_row[:, g], signs[:, g], 0.5, HEADS / 2 - 1.0, ALU.mult, ALU.add)\
                   .then_inc(deg_step, 1)
                dve.wait_ge(deg_step, 2 * n + 1)
                nc.vector.tensor_scalar(head_row[:, g], head_row[:, g], 0.0, None, ALU.max).then_inc(deg_step, 1)
                dve.wait_ge(deg_step, 2 * n + 2)
                nc.vector.tensor_copy(head_idx[:, g], head_row[:, g]).then_inc(rows_found, 1)

            def count_row(t):
                dve.wait_ge(level_got[t % 4], 16 * (t // 4 + 1))
                nc.vector.tensor_copy(h4[:, t, :], level[:, t % 4, 0:GE:P])
                if t > 0:
                    dve.wait_ge(level_done, t)
                nc.vector.tensor_scalar(level_junk[:, :], level[:, t % 4, :], ids[:, t:t + 1], None, ALU.is_le,
                                        ALU.add, accum_out=inner[:, t:t + 1]).then_inc(level_done, 1)

            between = [prepare_offsets, prepare_masks, prepare_max_mask, prepare_span]
            between += [lambda n=n: take(n) for n in range(BLOCKS)]
            between += [prepare_low, prepare_cell, prepare_columns]
            LAG = 4
            for t in range(TILES + LAG):
                if t < TILES and t % TG == 0:
                    find_rows(t // TG)
                if t >= LAG:
                    count_row(t - LAG)
                if t < len(between):
                    between[t]()
            dve.wait_ge(level_done, TILES)
            nc.vector.scalar_tensor_tensor(out=count[:, 1:TILES + 1], in0=head_row[:, :], scalar=float(GE),
                                           in1=inner[:, :], op0=ALU.mult, op1=ALU.add).then_inc(count_done, 1)
            dve.wait_ge(bias_spread, 1)
            nc.vector.tensor_copy(bias[:, :, :], bank_c[:, 0, :].rearrange("p (k f) -> p k f", k=4))\
              .then_inc(bias_kept, 1)
            prepare_way()
            assert steps[0] == PREP, steps

            dve.wait_ge(shifted, 1)
            dve.wait_ge(count_done, 2)
            nc.vector.tensor_tensor(indeg[:, :], count[:, 1:TILES + 1], bank_b[:, 0, 0:TILES], ALU.subtract)\
              .then_inc(deg_step, 1)
            n = 2 * TURNS + 1
            dve.wait_ge(deg_step, n)
            nc.vector.tensor_scalar(deg[:, :], indeg[:, :], 1.0, None, ALU.add).then_inc(deg_done, 1)
            nc.vector.tensor_scalar(has[:, :], indeg[:, :], 1.0, None, ALU.min)
            nc.vector.tensor_scalar(last_f[:, :], count[:, 1:TILES + 1], -1.0, 0.0, ALU.add, ALU.max)\
              .then_inc(deg_step, 1)
            dve.wait_ge(root_done, 1)
            nc.vector.reciprocal(dinv[:, :], sdeg[:, :]).then_inc(dinv_done, 1)
            dve.wait_ge(dinv_done, 1)
            dve.wait_ge(x_loaded, 32)
            for t in range(1, TILES, 2):
                nc.vector.tensor_scalar(own[:, t, :], xin[:, t, :], dinv[:, t:t + 1], None, ALU.mult)\
                   .then_inc(z_odd, 1)

            def first_windows(k):
                for s in range(SLOTS):
                    nc.vector.tensor_copy(idx_win[:, s, :], src_t[:, s * GC:(s + 1) * GC])\
                       .then_inc(win_ready[k], 1)

            dve.wait_ge(flip_copied, BLOCKS)
            dve.wait_ge(flip_kept, FLIPPED - BLOCKS)

            m = [0]

            def then(ins):
                ins.then_inc(idx_step, 1)
                m[0] += 1
                dve.wait_ge(idx_step, m[0])

            dve.wait_ge(short_spread, 1)
            then(nc.vector.tensor_copy(short_p[:, :], bank_c[:, 1, P:P + 1]))
            then(nc.vector.tensor_tensor(le4[:, :, :], h4[:, :, :],
                                         ids[:, :].rearrange("p (t c) -> p t c", c=1).to_broadcast([P, TILES, GC]),
                                         ALU.is_le))
            then(nc.vector.tensor_reduce(nle[:, :], le4[:, :, :], AX.X, ALU.add))
            then(nc.vector.tensor_tensor(h4[:, :, :], h4[:, :, :], le4[:, :, :], ALU.mult))
            then(nc.vector.tensor_reduce(first_dst[:, :], h4[:, :, :], AX.X, ALU.max))
            then(nc.vector.scalar_tensor_tensor(out=pos[:, :], in0=head_row[:, :], scalar=float(GC), in1=nle[:, :],
                                                op0=ALU.mult, op1=ALU.add))
            then(nc.vector.tensor_scalar(pos[:, :], pos[:, :], -1.0, 0.0, ALU.add, ALU.max))
            then(nc.vector.tensor_tensor(posd[:, :], ids[:, :], first_dst[:, :], ALU.subtract))
            then(nc.vector.tensor_scalar(posd[:, :], posd[:, :], WIN - 1.0, None, ALU.min))
            then(nc.vector.scalar_tensor_tensor(out=pos[:, :], in0=pos[:, :], scalar=float(WIN), in1=posd[:, :],
                                                op0=ALU.mult, op1=ALU.add))
            then(nc.vector.tensor_copy(last_i[:, :], last_f[:, :]))
            nc.vector.tensor_scalar(edge_i[:, :], last_i[:, :], P - 1, None, ALU.bitwise_and)
            then(nc.vector.tensor_scalar(chunk_i[:, :], last_i[:, :], GE - P, None, ALU.bitwise_and))
            then(nc.vector.scalar_tensor_tensor(out=last_f[:, :], in0=edge_i[:, :], scalar=GC - 1.0,
                                                in1=last_i[:, :], op0=ALU.mult, op1=ALU.add))
            then(nc.vector.scalar_tensor_tensor(out=last_f[:, :], in0=chunk_i[:, :], scalar=1.0 / P - 1.0,
                                                in1=last_f[:, :], op0=ALU.mult, op1=ALU.add))
            then(nc.vector.tensor_tensor(posd[:, :], pos[:, :], last_f[:, :], ALU.subtract))
            then(nc.vector.scalar_tensor_tensor(out=posd[:, :], in0=posd[:, :], scalar=short_p[:, 0:1],
                                                in1=last_f[:, :], op0=ALU.mult, op1=ALU.add))
            for w, t in ((0, posd), (1, last_f)):
                nc.vector.tensor_copy(last_idx[:, w, 0:TILES], t[:, :])
                then(nc.vector.tensor_copy(last_idx[:, w, TILES:TILES + 2 * TG], t[:, 0:2 * TG]))
            dve.wait_ge(bias_kept, 1)
            dve.wait_ge(z_even, (TILES + 1) // 2)
            dve.wait_ge(z_odd, TILES // 2)

            for k in range(3):
                op0, op1 = (ALU.mult, ALU.add) if k < 2 else (ALU.add, ALU.max)

                wait(dve, node_win_ready, k * WINDOWS)
                for h in range(2):
                    nc.vector.tensor_copy(node_win[:, h, :], last_idx[:, k // 2, h * TG:(h + 1) * TG])\
                       .then_inc(node_win_ready, 1)

                def short():
                    if k == 0:
                        dve.wait_ge(masks_stored, 48)

                    def next_window(i, h):
                        wait_alone(dve, turned[k], (i - 1) * UNITS)
                        nc.vector.tensor_copy(idx_turn[:, h, :], src_t[:, bass.ds(i * TURN_CH, POOL_CH)])\
                           .then_inc(win_ready[k], 1)

                    next_window(0, 0)

                    def table_parts(j):
                        n, step = j // 4, j % 4
                        g = slice(n * TG, (n + 1) * TG)
                        if n < TURNS and step == 1:
                            dve.wait_ge(part_hi[k], n + 1)
                            wait(dve, parts_done[k], n)
                            nc.vector.tensor_tensor(rest[:, :, :], own[:, g, :], parts[:, 0, g, :], ALU.subtract)\
                               .then_inc(rest_hi[k], 1)
                        if n < TURNS and step == 3:
                            dve.wait_ge(part_mid[k], n + 1)
                            dve.wait_ge(rest_hi[k], n + 1)
                            nc.vector.tensor_tensor(parts[:, 2, g, :], rest[:, :, :], parts[:, 1, g, :],
                                                    ALU.subtract).then_inc(parts_done[k], 1)

                    dve.wait_ge(iota_spread, k + 1)

                    def scan_gathered(i, h, pair, first):
                        dve.wait_ge(turned[k], UNITS * (i + 1))
                        dve.wait_ge(mask_here[k][h], 16 * (pair + 1))
                        wait(dve, turned_back[k], i - 1)
                        wait(dve, scanned[k], 2 * i)
                        init = 0.0 if first else scan[:, 1 - h, TC - 1:TC]
                        nc.vector.tensor_tensor_scan(scan[:, h, 0:PC], col_m[:, h, 0:PC], bank_d[:, 1, 0:PC], init,
                                                     op0, op1).then_inc(scanned[k], 1)

                    def scan_dense(i, h):
                        dve.wait_ge(applied[k], i + 1)
                        dve.wait_ge(scanned[k], 2 * i + 1)
                        nc.vector.tensor_tensor_scan(scan[:, h, PC:TC], col_m[:, h, PC:TC], bank_a[:, h, 0:DC],
                                                     scan[:, h, PC - 1:PC], op0, op1).then_inc(scanned[k], 1)

                    def turn(i, h, pair, first):
                        base = i * TURN_CH
                        wait(dve, turned[k], UNITS * (i - 1))
                        nc.vector.tensor_tensor(
                            hot_off[:, h, :, :],
                            off_t[:, bass.ds(base, POOL_CH)].rearrange("p (c l) -> p c l", l=1)
                            .to_broadcast([P, POOL_CH, WIN]),
                            iota_f[:, :].rearrange("p (a l) -> p a l", a=1).to_broadcast([P, POOL_CH, WIN]),
                            ALU.is_equal).then_inc(off_ready[k], 1)
                        for j in range(DENSE_CH):
                            c = base + (POOL_CH + j)
                            wait(dve, built[k], i * DENSE_CH + j - 3)
                            nc.vector.tensor_scalar(hot_low[:, j % 4, :], iota[:, MID:MID + P], low_t[:, bass.ds(c, 1)],
                                                    None, ALU.is_equal)
                            nc.vector.tensor_scalar(hot_cell[:, j % 4, 0:CELLS], iota, cell_t[:, bass.ds(c, 1)],
                                                    None, ALU.is_equal).then_inc(hot_ready[k], 1)
                            if isinstance(i, int) and i == 0:
                                table_parts(j)
                            elif j == 2:
                                if not first:
                                    scan_dense(i - 2, h)
                                scan_gathered(i - 1, 1 - h, pair if h == 1 else pair - 1,
                                              isinstance(i, int) and i == 1)
                            if j == 8 and not (isinstance(i, int) and i == FT - 1):
                                next_window(i + 1, 1 - h)

                    turn_pairs(dve, turn)
                    scan_dense(FT - 2, 1)
                    scan_gathered(FT - 1, 0, FT // 2, False)
                    scan_dense(FT - 1, 0)

                def general():
                    first_windows(k)
                    if k == 2:
                        dve.wait_ge(half_kept, TURNS)
                        for n in range(TURNS):
                            g = slice(n * TG, (n + 1) * TG)
                            nc.vector.tensor_tensor(own[:, g, :], own[:, g, :],
                                                    bias[:, 2:3, :].to_broadcast([P, TG, F]), ALU.add)\
                               .then_inc(half_biased, 1)

                    def body(i, first, last):
                        for s in range(SLOTS):
                            g = i * SLOTS + s
                            if not last:
                                wait_alone(dve, gathered[k][s], (i + 1) * 16 * GC)
                                nc.vector.tensor_copy(idx_win[:, s, :], src_t[:, bass.ds((g + SLOTS) * GC, GC)])\
                                   .then_inc(win_ready[k], 1)
                            dve.wait_ge(turned[k], g + 1)
                            dve.wait_ge(mask_here[k][s], (i + 1) * 16)
                            wait(dve, turned_back[k], g - 1)
                            wait(dve, scanned[k], g)
                            init = 0.0 if first and s == 0 else scan[:, (s - 1) % 2, GE - 1:GE]
                            nc.vector.tensor_tensor_scan(scan[:, s % 2, :], mask[:, s, :], bank_a[:, s % 2, :],
                                                         init, op0, op1).then_inc(scanned[k], 1)

                    turns(dve, ROUNDS, body)

                ways(dve, k, short, general)

                if k == 1:
                    dve.wait_ge(own_done, TURNS)
                elif k == 2:
                    dve.wait_ge(x1_kept, TURNS)
                    dve.wait_ge(half_biased, TURNS)

                def front(i, h, m):
                    n = i + k * TURNS
                    dve.wait_ge(node_gathered[h], (k * (TURNS // 2 + 1 - h) + m + 1) * 16 * TG)
                    wait(dve, agg_turned, n)
                    for j in range(TG):
                        t = i * TG + j
                        row = node_got[:, h, j, :]
                        if k < 2:
                            a = nc.vector.scalar_tensor_tensor(out=agg[:, j, :], in0=row,
                                                               scalar=has[:, bass.ds(t, 1)],
                                                               in1=one(own, t), op0=ALU.mult, op1=ALU.add)
                        else:
                            a = nc.vector.tensor_tensor(agg[:, j, :], row, bias[:, 3, :], ALU.add)
                    if k == 2:
                        a.then_inc(agg_pre, 1)
                        dve.wait_ge(agg_pre, i + 1)
                        for j in range(TG):
                            a = nc.vector.tensor_scalar(agg[:, j, :], agg[:, j, :], 0.0,
                                                        has[:, bass.ds(i * TG + j, 1)], ALU.max, ALU.mult)
                    a.then_inc(agg_made, 1)
                    nc.vector.tensor_copy(node_win[:, h, :], last_idx[:, k // 2, bass.ds((i + 2) * TG, TG)])\
                       .then_inc(node_win_ready, 1)

                def back(i, h, m):
                    n = i + k * TURNS
                    dve.wait_ge(linear_done, n + 1)
                    if k == 0:
                        wait(dve, tab_stored, n * 16)
                        wait(dve, own_done, i)
                        for j in range(TG):
                            t = i * TG + j
                            a = nc.vector.scalar_tensor_tensor(out=res[:, j, :], in0=nb[:, j, :],
                                                               scalar=dinv[:, bass.ds(t, 1)], in1=bias[:, 0, :],
                                                               op0=ALU.mult, op1=ALU.add)
                        a.then_inc(res_made, 1)
                        dve.wait_ge(res_made, n + 1)
                        for j in range(TG):
                            t = i * TG + j
                            a = nc.vector.tensor_scalar(tab[:, j, :], res[:, j, :], 0.0, dinv[:, bass.ds(t, 1)],
                                                        ALU.max, ALU.mult)
                        a.then_inc(tab_ready, 1)
                        return
                    old = xin[:, bass.ds(i * TG, TG), :]
                    if k == 1:
                        wait(dve, normed, i)
                    else:
                        wait(dve, tab_ready, n)
                    if k == 1:
                        if isinstance(i, int) and i == 0:
                            dve.wait_ge(x_loaded, 64)
                        for j in range(TG):
                            t = i * TG + j
                            a = nc.vector.scalar_tensor_tensor(out=res[:, j, :], in0=nb[:, j, :],
                                                               scalar=dinv[:, bass.ds(t, 1)], in1=one(xin, t),
                                                               op0=ALU.mult, op1=ALU.add)
                        a.then_inc(res_pre, 1)
                        dve.wait_ge(res_pre, i + 1)
                        nc.vector.tensor_tensor(res[:, :, :], res[:, :, :], bias[:, 1:2, :].to_broadcast([P, TG, F]),
                                                ALU.add).then_inc(res_made, 1)
                    else:
                        nc.vector.tensor_tensor(res[:, :, :], nb, own[:, bass.ds(i * TG, TG), :], ALU.add)\
                           .then_inc(res_pre, 1)
                        dve.wait_ge(res_pre, i + TURNS + 1)
                        nc.vector.scalar_tensor_tensor(out=res[:, :, :], in0=res[:, :, :], scalar=0.0, in1=old,
                                                       op0=ALU.max, op1=ALU.add).then_inc(res_made, 1)
                    dve.wait_ge(res_made, n + 1)
                    m = i + (k - 1) * TURNS
                    for j in range(TG):
                        nc.vector.bn_stats(stats[:, j, :], res[:, j, :]).then_inc(stats_made, 1)
                    wait_alone(dve, stats_made, m * TG + TG)
                    for j in range(TG):
                        nc.vector.bn_aggr(mv[:, j, :], stats[:, j, :]).then_inc(mv_made, 1)
                    dve.wait_ge(sd_made, m + 1)
                    nc.vector.reciprocal(rstd[:, :], sd[:, :]).then_inc(rstd_made, 1)
                    dve.wait_ge(rstd_made, m + 1)
                    if k == 2:
                        wait(dve, tab_stored, n * 16)
                    else:
                        wait(dve, x1_kept, i)
                        wait(dve, x1_turned, i)
                    for j in range(TG):
                        to = xn[:, j, :] if k == 1 else tab[:, j, :]
                        a = nc.vector.tensor_scalar(to, res[:, j, :], mv[:, j, 0:1], rstd[:, j:j + 1],
                                                    ALU.subtract, ALU.mult)
                    a.then_inc(normed if k == 1 else tab_ready, 1)

                node_steps(dve, front, back)


_INS = ["x", "src", "dst", "edge_weight", "L0_gnn_W1", "L0_gnn_b1", "L0_gnn_W2", "L0_gnn_b2",
        "L1_gnn_pool_w", "L1_gnn_pool_b", "L1_gnn_final_w", "L1_gnn_final_b"]


def kernel(**inputs):
    import numpy as _np
    import concourse.bacc as _bacc
    from concourse import mybir as _mybir
    from concourse.bass_utils import run_bass_kernel_spmd as _run

    nc = _bacc.Bacc("TRN2", target_bir_lowering=False, num_devices=1)
    arrays, args = {}, []
    for name in _INS:
        a = _np.ascontiguousarray(inputs[name])
        arrays[f"in_{name}"] = a
        args.append(nc.dram_tensor(f"in_{name}", a.shape, _mybir.dt.from_np(a.dtype), kind="ExternalInput").ap())
    result = nc.dram_tensor("out_0", (NODES, F), F32, kind="ExternalOutput").ap()
    program(nc, *args, result)
    r = _run(nc, [arrays], core_ids=[0])
    return r.results[0]["out_0"]
```
